# Optimizing a Trainium2 kernel written in Bass

```python
import numpy as np
import jax
import jax.numpy as jnp

def _softmax(x, axis=-1):
    return jax.nn.softmax(x, axis=axis)

def _gelu(x):
    return jax.nn.gelu(x, approximate=True)

def _silu(x):
    return jax.nn.silu(x)

def _sigmoid(x):
    return jax.nn.sigmoid(x)

def _layernorm(x, axis=-1, eps=1e-05):
    m = jnp.mean(x, axis=axis, keepdims=True)
    v = jnp.var(x, axis=axis, keepdims=True)
    return (x - m) / jnp.sqrt(v + eps)

def _scatter_add(tgt, idx, src, axis=0):
    return tgt.at[idx].add(src)

def _segment_sum(src, seg, n):
    return jax.ops.segment_sum(src, seg, n)
kernel_name = 'mk_audio_tower_d1_tok_audfeat512_r4_6cce78'

def setup_inputs(seed: int=0):
    np.random.seed(seed)
    _w = jnp.asarray

    def _rec_inputs():
        import jax
        import jax.numpy as jnp
        _rk = jax.random.key(seed)
        x = -7.10856e-05 + 0.999911 * jax.random.normal(jax.random.fold_in(_rk, 1), (64, 750, 128), jnp.float32)
        return x
    x = _rec_inputs()

    def _L0_tok_setup():
        import jax, jax.numpy as jnp
        import numpy as np
        import math
        B, T, D = (32, 1024, 128)
        P, S = (16, 8)
        E = 128

        def _compute_patch_pad(T, P, S):
            if T <= 0:
                return 0
            if T < P:
                return P - T
            n_patches = math.ceil((T - P) / S) + 1
            return max(0, (n_patches - 1) * S + P - T)
        key = jax.random.key(seed)
        k1, k2, k3 = jax.random.split(key, 3)
        x = jax.random.normal(k1, (B, T, D), dtype=jnp.float32)
        bound = 1.0 / math.sqrt(P * D)
        W = jax.random.uniform(k2, (E, P * D), dtype=jnp.float32, minval=-bound, maxval=bound)
        b = jax.random.uniform(k3, (E,), dtype=jnp.float32, minval=-bound, maxval=bound)
        return {'x': x, 'W': W, 'b': b}
    _L0_tok_all = _L0_tok_setup()
    _L0_tok_in = {k: v for k, v in _L0_tok_all.items() if k in ('W', 'b')}
    del _L0_tok_all

    def _L0_attn_setup():
        import jax, jax.numpy as jnp
        import numpy as np
        import math
        DIM = 128
        HEADS = 8
        DIM_HEAD = 64
        INNER = HEADS * DIM_HEAD
        B = 2
        N = 512

        def _alibi_slopes(heads):

            def pow2(n):
                start = 2 ** (-2 ** (-(math.log2(n) - 3)))
                return [start * start ** i for i in range(n)]
            if math.log2(heads).is_integer():
                return pow2(heads)
            cp2 = 2 ** math.floor(math.log2(heads))
            return pow2(cp2) + pow2(2 * cp2)[0::2][:heads - cp2]

        def _proj(xp, w1, wd):
            y = jnp.einsum('ed,bdn->ben', w1, xp)
            y = wd[None, :, 0:1] * y[..., :-2] + wd[None, :, 1:2] * y[..., 1:-1] + wd[None, :, 2:3] * y[..., 2:]
            return y

        def _split_heads(y, b, n):
            return y.reshape(b, HEADS, DIM_HEAD, n).transpose(0, 1, 3, 2)
        key = jax.random.key(seed)
        ks = jax.random.split(key, 9)
        s = 0.02
        return {'x': jax.random.normal(ks[0], (B, N, DIM), dtype=jnp.float32), 'gamma': jnp.ones((DIM,), jnp.float32), 'beta': jnp.zeros((DIM,), jnp.float32), 'wq1': jax.random.normal(ks[1], (INNER, DIM), jnp.float32) * s, 'wqd': jax.random.normal(ks[2], (INNER, 3), jnp.float32) * s, 'wk1': jax.random.normal(ks[3], (INNER, DIM), jnp.float32) * s, 'wkd': jax.random.normal(ks[4], (INNER, 3), jnp.float32) * s, 'wv1': jax.random.normal(ks[5], (INNER, DIM), jnp.float32) * s, 'wvd': jax.random.normal(ks[6], (INNER, 3), jnp.float32) * s, 'wout': jax.random.normal(ks[7], (DIM, INNER), jnp.float32) * s}
    _L0_attn_all = _L0_attn_setup()
    _L0_attn_in = {k: v for k, v in _L0_attn_all.items() if k in ('gamma', 'beta', 'wq1', 'wqd', 'wk1', 'wkd', 'wv1', 'wvd', 'wout')}
    del _L0_attn_all

    def _L0_ffn_setup():
        import jax, jax.numpy as jnp
        import numpy as np
        TOP_K = 2
        key = jax.random.key(seed)
        k1, k2, k3, k4 = jax.random.split(key, 4)
        B, S, D, F, E = (4, 128, 128, 512, 16)
        hidden_states = jax.random.normal(k1, (B, S, D), dtype=jnp.float32)
        gate_weight = jax.random.normal(k2, (E, D), dtype=jnp.float32) * 0.02
        w1 = jax.random.normal(k3, (E, F, D), dtype=jnp.float32) * 0.02
        w2 = jax.random.normal(k4, (E, D, F), dtype=jnp.float32) * 0.02
        return {'hidden_states': hidden_states, 'gate_weight': gate_weight, 'w1': w1, 'w2': w2}
    _L0_ffn_all = _L0_ffn_setup()
    _L0_ffn_in = {k: v for k, v in _L0_ffn_all.items() if k in ('gate_weight', 'w1', 'w2')}
    del _L0_ffn_all
    return {'x': x, 'L0_tok_W': _L0_tok_in['W'], 'L0_tok_b': _L0_tok_in['b'], 'L0_attn_gamma': _L0_attn_in['gamma'], 'L0_attn_beta': _L0_attn_in['beta'], 'L0_attn_wq1': _L0_attn_in['wq1'], 'L0_attn_wqd': _L0_attn_in['wqd'], 'L0_attn_wk1': _L0_attn_in['wk1'], 'L0_attn_wkd': _L0_attn_in['wkd'], 'L0_attn_wv1': _L0_attn_in['wv1'], 'L0_attn_wvd': _L0_attn_in['wvd'], 'L0_attn_wout': _L0_attn_in['wout'], 'L0_ffn_gate_weight': _L0_ffn_in['gate_weight'], 'L0_ffn_w1': _L0_ffn_in['w1'], 'L0_ffn_w2': _L0_ffn_in['w2']}

def reference(x, L0_tok_W, L0_tok_b, L0_attn_gamma, L0_attn_beta, L0_attn_wq1, L0_attn_wqd, L0_attn_wk1, L0_attn_wkd, L0_attn_wv1, L0_attn_wvd, L0_attn_wout, L0_ffn_gate_weight, L0_ffn_w1, L0_ffn_w2):
    import jax
    import jax.numpy as jnp

    def _L0_tok_ref(x, W, b):
        import jax, jax.numpy as jnp
        import numpy as np
        import math
        B, T, D = (32, 1024, 128)
        P, S = (16, 8)
        E = 128

        def _compute_patch_pad(T, P, S):
            if T <= 0:
                return 0
            if T < P:
                return P - T
            n_patches = math.ceil((T - P) / S) + 1
            return max(0, (n_patches - 1) * S + P - T)
        Bx, Tx, Dx = x.shape
        pad = _compute_patch_pad(Tx, P, S)
        if pad > 0:
            x = jnp.pad(x, ((0, 0), (0, pad), (0, 0)))
        T_pad = x.shape[1]
        Np = (T_pad - P) // S + 1
        idx = jnp.arange(Np)[:, None] * S + jnp.arange(P)[None, :]
        patches = x[:, idx, :]
        Wr = W.reshape(E, Dx, P)
        tokens = jnp.einsum('bnpd,edp->bne', patches, Wr) + b
        return tokens

    def _L0_attn_ref(x, gamma, beta, wq1, wqd, wk1, wkd, wv1, wvd, wout):
        import jax, jax.numpy as jnp
        import numpy as np
        import math
        DIM = 128
        HEADS = 8
        DIM_HEAD = 64
        INNER = HEADS * DIM_HEAD
        B = 2
        N = 512

        def _alibi_slopes(heads):

            def pow2(n):
                start = 2 ** (-2 ** (-(math.log2(n) - 3)))
                return [start * start ** i for i in range(n)]
            if math.log2(heads).is_integer():
                return pow2(heads)
            cp2 = 2 ** math.floor(math.log2(heads))
            return pow2(cp2) + pow2(2 * cp2)[0::2][:heads - cp2]

        def _proj(xp, w1, wd):
            y = jnp.einsum('ed,bdn->ben', w1, xp)
            y = wd[None, :, 0:1] * y[..., :-2] + wd[None, :, 1:2] * y[..., 1:-1] + wd[None, :, 2:3] * y[..., 2:]
            return y

        def _split_heads(y, b, n):
            return y.reshape(b, HEADS, DIM_HEAD, n).transpose(0, 1, 3, 2)
        b, n, d = x.shape
        scale = DIM_HEAD ** (-0.5)
        mu = jnp.mean(x, axis=-1, keepdims=True)
        var = jnp.var(x, axis=-1, keepdims=True)
        xn = (x - mu) / jnp.sqrt(var + 1e-05) * gamma + beta
        xp = jnp.pad(xn.transpose(0, 2, 1), ((0, 0), (0, 0), (2, 0)))
        q = _split_heads(_proj(xp, wq1, wqd), b, n) * scale
        k = _split_heads(_proj(xp, wk1, wkd), b, n)
        v = _split_heads(_proj(xp, wv1, wvd), b, n)
        sim = jnp.einsum('bhid,bhjd->bhij', q, k)
        slopes = jnp.asarray(_alibi_slopes(HEADS), dtype=sim.dtype)
        idx = jnp.arange(n)
        bias = -jnp.abs(idx[None, :] - idx[:, None]).astype(sim.dtype)
        sim = sim + bias[None, None] * slopes[None, :, None, None]
        causal = jnp.triu(jnp.ones((n, n), bool), 1)
        sim = jnp.where(causal[None, None], -jnp.finfo(sim.dtype).max, sim)
        attn = jax.nn.softmax(sim, axis=-1)
        out = jnp.einsum('bhij,bhjd->bhid', attn, v)
        out = out.transpose(0, 2, 1, 3).reshape(b, n, INNER)
        return out @ wout.T

    def _L0_ffn_ref(hidden_states, gate_weight, w1, w2):
        import jax, jax.numpy as jnp
        import numpy as np
        TOP_K = 2
        B, S, D = hidden_states.shape
        E = gate_weight.shape[0]
        x = hidden_states.reshape(-1, D)
        gate_logits = x @ gate_weight.T
        top_vals, top_idx = jax.lax.top_k(gate_logits, TOP_K)
        routing_w = jax.nn.softmax(top_vals, axis=-1)
        mask = jnp.any(top_idx[:, :, None] == jnp.arange(E)[None, None, :], axis=1)
        h = jax.nn.silu(jnp.einsum('td,efd->tef', x, w1))
        counts = jnp.sum(mask, axis=0)
        h_sum = jnp.einsum('tef,te->ef', h, mask.astype(h.dtype))
        h_mean = h_sum / jnp.maximum(counts, 1)[:, None].astype(h.dtype)
        y_mean = jnp.einsum('ef,edf->ed', h_mean, w2)
        y_mean = jnp.where((counts > 0)[:, None], y_mean, 0.0)
        out = jnp.einsum('tk,tkd->td', routing_w, y_mean[top_idx])
        return out.reshape(B, S, D)
    h = _L0_tok_ref(x, L0_tok_W, L0_tok_b)
    h = h + _L0_attn_ref(_layernorm(h, axis=-1), L0_attn_gamma, L0_attn_beta, L0_attn_wq1, L0_attn_wqd, L0_attn_wk1, L0_attn_wkd, L0_attn_wv1, L0_attn_wvd, L0_attn_wout)
    h = h + _L0_ffn_ref(_layernorm(h, axis=-1), L0_ffn_gate_weight, L0_ffn_w1, L0_ffn_w2)
    return h

_drawn_inputs = setup_inputs


def setup_inputs(seed=0):
    import zlib

    import numpy as np

    out = dict(_drawn_inputs(seed))
    spreads = {'L0_attn_gamma': (1.0, 0.6), 'L0_attn_beta': (0.0, 0.8)}
    factors = {'L0_attn_wq1': 8.0,
     'L0_attn_wqd': 8.0,
     'L0_attn_wk1': 8.0,
     'L0_attn_wkd': 8.0,
     'L0_attn_wv1': 8.0,
     'L0_attn_wvd': 8.0,
     'L0_attn_wout': 8.0,
     'L0_ffn_gate_weight': 4.966,
     'L0_ffn_w1': 6.077,
     'L0_ffn_w2': 4.783}
    for name, (base, spread) in spreads.items():
        noise = np.random.default_rng([zlib.crc32(name.encode()), seed]).standard_normal(out[name].shape)
        drawn = base * np.exp(spread * noise) if base else spread * noise
        out[name] = jnp.asarray(drawn.astype(out[name].dtype))
    for name, factor in factors.items():
        out[name] = (out[name] * factor).astype(out[name].dtype)
    return out
```

```python
from contextlib import ExitStack

import concourse.bass as bass
from concourse import mybir

F32 = mybir.dt.float32
BF16 = mybir.dt.bfloat16
I32 = mybir.dt.int32
U32 = mybir.dt.uint32
ALU = mybir.AluOpType
ACT = mybir.ActivationFunctionType
AXX = mybir.AxisListType.X

B, T, D = 64, 750, 128
P, S = 16, 8
NT = 93
MR = NT + 1
H, DH = 8, 64
E, F = 16, 512
EPS = 1e-5
GB = 4
NG = B // GB
GT = GB * NT
QB = H * DH // 128
NBLK = 3 * QB
CAP = B * NT + 128
ROWS = E * CAP + 128
NTILE = (2 * B * NT + E * 127) // 128
FB = F // 128
ESTRIDE = 32

C_IOTA, C_BASE, C_TILE, C_BLK, C_HOT, C_END = 0, E, 2 * E, 2 * E + 1, 2 * E + 1 + GB, 2 * E + 1 + GB + 2 * E - 1


def build(nc, x, w_tok, b_tok, gamma, beta, wq, wk, wv, cq, ck, cv, w_out, w_gate, w1, w2,
          c_ident, c_bias, c_tri, c_misc, out):
    rows = nc.dram_tensor("expert_rows", [ROWS, D], F32, kind="Internal").ap()
    ctx = ExitStack()
    with ctx:
        def sb(name, shape, dt=F32):
            return ctx.enter_context(nc.sbuf_tensor(name, shape, dt))

        def sem(name):
            return ctx.enter_context(nc.semaphore(name))

        wtok = sb("wtok", [D, P, D])
        btok = sb("btok", [D, 1])
        gam = sb("gam", [D, 1])
        bet = sb("bet", [D, 1])
        wqkv = sb("wqkv", [D, NBLK, 128])
        taps = sb("taps", [D, NBLK, 3])
        wout = sb("wout", [128, QB, D])
        wgate = sb("wgate", [D, E])
        w1s = sb("w1s", [D, E * F])
        w2s = sb("w2s", [128, FB, E, D])
        ident = sb("ident", [128, 128])
        bias = sb("bias", [NT, 2, GT], BF16)
        ident16 = sb("ident16", [128, 128], BF16)
        tri = sb("tri", [NT, NT], BF16)
        ones16 = sb("ones16", [NT, 128], BF16)
        misc = sb("misc", [128, C_END])
        half = sb("half", [NT, GB])
        zeros = sb("zeros", [128, D])
        xbuf = [sb(f"xbuf{u}", [D, GB, S, MR]) for u in range(2)]
        tokT = sb("tokT", [D, GT])
        resid = sb("resid", [NT, B * D])
        stat = sb("stat", [NT, GB, 6])
        mv = sb("mv", [NT, GB, 2])
        veps = sb("veps", [NT, GB])
        rstd = sb("rstd", [NT, GB])
        xn = sb("xn", [NT, GB, D])
        xnT = sb("xnT", [D, GT])
        qkv = [sb(f"qkv{u}", [128, NBLK, GB, NT]) for u in range(2)]
        early = qkv[1][:].rearrange("p k b n -> p (k b n)")
        bias32, tri32 = early[:NT, 0:2 * GT], early[:NT, 2 * GT:2 * GT + NT]
        vrow = [sb(f"vrow{u}", [NT, H, DH + 1]) for u in range(2)]
        rmax = sb("rmax", [NT, 2, 4])
        prob = sb("prob", [NT, 2, 4, NT])
        probT = sb("probT", [NT, 2, 4, NT])
        rden = sb("rden", [NT, 2, 4])
        attn = sb("attn", [NT, H * DH])
        attnT = sb("attnT", [128, QB, NT])
        stat2 = sb("stat2", [NT, GB, 6])
        mv2 = sb("mv2", [NT, GB, 2])
        veps2 = sb("veps2", [NT, GB])
        rstd2 = sb("rstd2", [NT, GB])
        hn = [sb(f"hn{u}", [NT, GB, D]) for u in range(2)]
        hnT = sb("hnT", [D, GT])
        logit = sb("logit", [NT, GB, E])
        top = sb("top", [NT, GB, 8])
        topi = sb("topi", [NT, GB, 8], U32)
        idxf = sb("idxf", [NT, 2, GB])
        hot = sb("hot", [NT, 2 * GB, E])
        mask = sb("mask", [NT, GB * E], BF16)
        gap = sb("gap", [NT, GB])
        egap = sb("egap", [NT, GB])
        wts = sb("wts", [NT, 2, GB])
        wden = sb("wden", [NT, GB])
        base = [sb(f"base{u}", [128, E]) for u in range(2)]
        pos = sb("pos", [NT, GB * E])
        sel = sb("sel", [NT, 2 * GB, E])
        slot = [sb(f"slot{u}", [NT, 2 * GB], I32) for u in range(2)]
        slotf = sb("slotf", [NT, 2 * GB])
        wsel = sb("wsel", [NT, 2 * GB, E])
        rw = sb("rw", [NT, GB, ESTRIDE])
        rwT = sb("rwT", [128, NG * NT])
        cnt = sb("cnt", [128, E])
        cnti = sb("cnti", [128, E], I32)
        cntt = sb("cntt", [128, E], I32)
        tcol = sb("tcol", [128, 8])
        taili = sb("taili", [1, E], I32)
        NX = 4
        late = [qkv[u][:].rearrange("p k b n -> p (k b n)") for u in range(2)]
        xs = [late[0][:, k * D:(k + 1) * D] for k in range(NX)]
        xsT = [late[0][:, (NX + k) * 128:(NX + k + 1) * 128] for k in range(2)]
        act = [late[0][:, (NX + 2) * 128 + k * F:(NX + 2) * 128 + (k + 1) * F] for k in range(2)]
        osb = [late[1][:NT, u * GB * D:(u + 1) * GB * D] for u in range(2)]
        ymix = late[1][:, 2 * GB * D:3 * GB * D].rearrange("p (b d) -> p b d", d=D)
        spare = late[1][:, 3 * GB * D:]
        hsum = spare[:, 0:FB * E]
        yT = spare[:, 64:64 + GB * ESTRIDE].rearrange("p (b e) -> p b e", e=ESTRIDE)
        rstage = [spare[:, 192 + u * NT:192 + (u + 1) * NT] for u in range(2)]
        tab = spare[0:1, 500:500 + 3 * 128].bitcast(I32)
        ntl, ones, tend, past, pastt, invc = (spare[:, 400 + k * E:400 + (k + 1) * E] for k in range(6))

        ps = [ctx.enter_context(nc.psum_tensor(f"ps{i}", [128, 512], F32)) for i in range(3)]
        psTok, psP = ps[0], ps[1:3]
        psS = ctx.enter_context(nc.psum_tensor("psS", [128, 2, 512], F32))
        psO = ctx.enter_context(nc.psum_tensor("psO", [128, 2, 512], F32))
        psV = ctx.enter_context(nc.psum_tensor("psV", [128, 512], F32))
        psWout = psO[:NT, 0, 384:512]
        psTot = psO[:, 0, 264:264 + E]
        psRT = psV[:, 384:384 + NT]
        psHn = psO[:, 1, 0:GT]
        psGate = psO[:NT, 1, 384:448]
        psRank = psO[:NT, 1, 448:512]

        x_in = [sem(f"x_in{u}") for u in range(2)]
        tok_w_in, small_in, proj_w_in, expert_w_in, zero_tile_out = (
            sem("tok_w_in"), sem("small_in"), sem("proj_w_in"), sem("expert_w_in"), sem("zero_tile_out"))
        consts_ready, zeros_ready, taps_ready, bias_cast, vones_ready, rwzero_ready = (
            sem("consts_ready"), sem("zeros_ready"), sem("taps_ready"), sem("bias_cast"),
            sem("vones_ready"), sem("rwzero_ready"))
        tok_mm, tok_evac, tok_tr, res_evac = sem("tok_mm"), sem("tok_evac"), sem("tok_tr"), sem("res_evac")
        ln_stat, ln_mv, ln_veps, ln_rstd, xn_ready = (
            sem("ln_stat"), sem("ln_mv"), sem("ln_veps"), sem("ln_rstd"), sem("xn_ready"))
        xnT_tr, xnT_evac = sem("xnT_tr"), sem("xnT_evac")
        proj_mm, tap2_done, tap1_done, conv_done = (
            sem("proj_mm"), sem("tap2_done"), sem("tap1_done"), sem("conv_done"))
        v_tr, v_evac, s_mm, max_done, shift_done, exp_done = (
            sem("v_tr"), sem("v_evac"), sem("s_mm"), sem("max_done"), sem("shift_done"), sem("exp_done"))
        p_tr, p_evac, pv_mm, den_done, norm_done = (
            sem("p_tr"), sem("p_evac"), sem("pv_mm"), sem("den_done"), sem("norm_done"))
        a_tr, a_evac, out_mm, res_add = sem("a_tr"), sem("a_evac"), sem("out_mm"), sem("res_add")
        ln2_stat, ln2_mv, ln2_veps, ln2_rstd, hn_ready = (
            sem("ln2_stat"), sem("ln2_mv"), sem("ln2_veps"), sem("ln2_rstd"), sem("hn_ready"))
        hnT_tr, hnT_evac, gate_mm, logit_copy, top_done, topi_done, idxf_done = (
            sem("hnT_tr"), sem("hnT_evac"), sem("gate_mm"), sem("logit_copy"), sem("top_done"),
            sem("topi_done"), sem("idxf_done"))
        hot_done, mask_done, gap_done, egap_done, wden_done, w0_done, w1_done = (
            sem("hot_done"), sem("mask_done"), sem("gap_done"), sem("egap_done"), sem("wden_done"),
            sem("w0_done"), sem("w1_done"))
        rank_mm, pos_done, base_done, sel_done, slotf_done, slot_done, wsel_done, rw_done = (
            sem("rank_mm"), sem("pos_done"), sem("base_done"), sem("sel_done"), sem("slotf_done"), sem("slot_done"),
            sem("wsel_done"), sem("rw_done"))
        rwT_tr, rwT_evac = sem("rwT_tr"), sem("rwT_evac")
        scattered = sem("scattered")
        dve_step, tcol_ready, table_mm, table_ready, tail_ready, tails_out = (
            sem("dve_step"), sem("tcol_ready"), sem("table_mm"), sem("table_ready"), sem("tail_ready"), sem("tails_out"))
        xs_in = [sem(f"xs_in{k}") for k in range(NX)]
        xs_tr, xs_evac, up_mm, silu_done, sum_mm = (
            sem("xs_tr"), sem("xs_evac"), sem("up_mm"), sem("silu_done"), sem("sum_mm"))
        hsum_evac, down_mm, y_scaled, yT_tr, ymix_ready = (
            sem("hsum_evac"), sem("down_mm"), sem("y_scaled"), sem("yT_tr"), sem("ymix_ready"))
        rstage_done, mix_mm, out_add = sem("rstage_done"), sem("mix_mm"), sem("out_add")
        out_done = [sem(f"out_done{u}") for u in range(2)]

        iota = misc[:NT, C_IOTA:C_IOTA + E]
        hotrow = misc[:, C_HOT:C_END]

        def heads(psum, width):
            return psum[:NT, :, 0:4 * width].rearrange("p a (h c) -> p a h c", c=width)

        def wait(eng, s, value):
            if isinstance(value, int) and value <= 0:
                return
            eng.wait_ge(s, value)

        passed = sem("passed")

        def wait_apart(eng, s, value):
            wait(eng, s, value)
            if not isinstance(value, int):
                eng.sem_inc(passed, 1)

        class Stage:
            def __init__(self, tok, proj, attn, last, gate, scat):
                self.tok, self.proj, self.attn, self.last, self.gate, self.scat = tok, proj, attn, last, gate, scat

        def stages(t):
            return Stage(t < NG, 0 <= t - 1 < NG, 0 <= t - 2 < NG, 0 <= t - 3 < NG, 0 <= t - 3 < NG,
                         0 <= t - 4 < NG)

        FULL = Stage(True, True, True, True, True, True)
        LOOP_FROM, LOOP_PAIRS = 5, (NG - 5) // 2
        LAST_T = NG + 3

        def run(eng, step):
            for t in range(LOOP_FROM):
                step(t, t % 2, stages(t))
            with eng.Fori(0, LOOP_PAIRS) as r:
                for t in range(LOOP_FROM, LOOP_FROM + 2):
                    step(r * 2 + t, t % 2, FULL)
            for t in range(LOOP_FROM + 2 * LOOP_PAIRS, LAST_T + 1):
                step(t, t % 2, stages(t))

        PROJ = {(1, 1): (0, 1), (2, 0): (2, 3), (2, 1): (4, 5, 6), (3, 0): (7, 8), (3, 1): (9, 10, 11)}

        block = ctx.enter_context(nc.Block())

        @block.sync
        def _(sp):
            sp.dma_start(xbuf[0][:].rearrange("p b r m -> p (b r m)"), x[:, bass.ds(0, GB * S * MR)]).then_inc(x_in[0], 16)
            sp.dma_start(xbuf[1][:].rearrange("p b r m -> p (b r m)"), x[:, bass.ds(GB * S * MR, GB * S * MR)]).then_inc(x_in[1], 16)
            for dst, src in ((wqkv[:, 0:QB, :], wq), (wqkv[:, QB:2 * QB, :], wk), (wqkv[:, 2 * QB:, :], wv),
                             (taps[:, 0:QB, :], cq), (taps[:, QB:2 * QB, :], ck), (taps[:, 2 * QB:, :], cv),
                             (wout[:, :, :], w_out), (wgate[:, :], w_gate)):
                sp.dma_start(dst, src).then_inc(proj_w_in, 16)
            with sp.Fori(0, (NG - 2) // 2) as r:
                for u in range(2):
                    sp.wait_ge(tok_mm, r * 2 + (u + 1))
                    sp.dma_start(xbuf[u][:].rearrange("p b r m -> p (b r m)"),
                                 x[:, bass.ds((r * 2 + (u + 2)) * (GB * S * MR), GB * S * MR)]).then_inc(x_in[u], 16)
            sp.wait_ge(zeros_ready, 1)
            sp.dma_start(rows[E * CAP:ROWS, :], zeros[:, :]).then_inc(zero_tile_out, 16)
            sp.wait_ge(tail_ready, 1)
            for e in range(E):
                start = sp.value_load(taili[0:1, e:e + 1], min_val=0, max_val=E * CAP)
                sp.dma_start(rows[bass.ds(start, 128), :], zeros[:, :]).then_inc(tails_out, 16)
            sp.wait_ge(table_ready, 1)
            sp.wait_ge(scattered, 16 * 2 * B)
            sp.wait_ge(zero_tile_out, 16)
            sp.wait_ge(tails_out, 16 * E)
            def fetch(i, k):
                start = sp.value_load(tab[0:1, bass.ds(i, 1)], min_val=0, max_val=E * CAP)
                wait(sp, xs_tr, i - (NX - 1))
                sp.dma_start(xs[k][:, :], rows[bass.ds(start, 128), :]).then_inc(xs_in[k], 16)

            for k in range(NX):
                fetch(k, k)
            with sp.Fori(1, NTILE // NX) as r:
                for k in range(NX):
                    fetch(r * NX + k, k)
            with sp.Fori(0, NG // 2) as r:
                for u in range(2):
                    sp.wait_ge(out_add, r * 2 + (u + 1))
                    sp.dma_start(out[bass.ds((r * 2 + u) * GB, GB), :, :].rearrange("b t d -> t b d"),
                                 osb[u][:, :].rearrange("t (b d) -> t b d", d=D)).then_inc(out_done[u], 16)
            sp.wait_ge(out_done[0], 16 * (NG // 2))
            sp.wait_ge(out_done[1], 16 * (NG // 2))
            sp.wait_ge(expert_w_in, 32)

        @block.tensor
        def _(pe):
            pe.wait_ge(tok_w_in, 16)
            pe.wait_ge(small_in, 16 * 7)

            def tok_taps(t, u, first, count):
                if first == 0:
                    wait(pe, x_in[u], (t - u) * 8 + 16)
                    wait(pe, tok_evac, t)
                for p in range(first, first + count):
                    r, m = p % S, p // S
                    mm = nc.tensor.matmul(psTok[:, 0:GT], wtok[:, p, :], xbuf[u][:, :, r, m:m + NT],
                                          start=(p == 0), stop=(p == P - 1))
                if first + count == P:
                    mm.then_inc(tok_mm, 1)

            def proj(t, k):
                if k == 0:
                    wait(pe, xnT_evac, t)
                    if isinstance(t, int) and t == 1:
                        pe.wait_ge(proj_w_in, 16 * 8)
                if k >= 2:
                    wait(pe, conv_done, (t - 1) * NBLK + (k - 1))
                nc.tensor.matmul(psP[k % 2][:, 0:GT], wqkv[:, k, :], xnT[:, :], start=True,
                                 stop=True).then_inc(proj_mm, 1)

            def step(t, u, f):
                for s in range(GB):
                    n = (t - 2) * GB + s
                    prev = f.attn and s > 0 or f.last and s == 0
                    if prev:
                        pe.wait_ge(exp_done, n)
                        for a in range(2):
                            for hh in range(4):
                                mm = nc.tensor.transpose(psS[:NT, a, hh * NT:(hh + 1) * NT], prob[:, a, hh, :],
                                                         ident[:NT, :NT])
                            mm.then_inc(p_tr, 1)
                    if f.attn:
                        if s == 0:
                            pe.wait_ge(conv_done, (t - 1) * NBLK)
                        wait(pe, a_evac, n - 1)
                        for j in range(QB):
                            mm = nc.tensor.transpose(psV[:NT, j * 128:(j + 1) * 128],
                                                     qkv[u][:, 2 * QB + j, s, :], ident[:, :])
                        mm.then_inc(v_tr, 1)
                    if f.tok:
                        tok_taps(t, u, 4 * s, 2)
                    if f.attn:
                        if s == 0 and isinstance(t, int) and t == 2:
                            pe.wait_ge(bias_cast, 3)
                        wait(pe, p_evac, n * 2)
                        for a in range(2):
                            nc.tensor.matmul(psS[:NT, a, 0:4 * NT], ident16[:NT, :NT], bias[:, a, :],
                                             start=True, stop=False, skip_group_check=True)
                        for hh in range(4):
                            for a in range(2):
                                lo = 64 * a
                                mm = nc.tensor.matmul(psS[:NT, a, hh * NT:(hh + 1) * NT],
                                                      qkv[u][lo:lo + 64, hh, s, :], qkv[u][lo:lo + 64, QB + hh, s, :],
                                                      start=False, stop=True, skip_group_check=True)
                        mm.then_inc(s_mm, 1)
                    if prev:
                        pe.wait_ge(p_evac, n * 2)
                        pe.wait_ge(v_evac, n)
                        wait(pe, norm_done, n - 1)
                        wait(pe, res_add, n - 1)
                        if f.gate and s == 2:
                            wait(pe, hnT_evac, t - 2)
                        if f.gate and s == 3:
                            wait(pe, logit_copy, t - 2)
                        if f.scat and s == 0:
                            wait(pe, pos_done, t - 3)
                        for h in range(H):
                            mm = nc.tensor.matmul(psO[:NT, h // 4, (h % 4) * (DH + 1):(h % 4 + 1) * (DH + 1)],
                                                  probT[:, h % 2, h // 2, :], vrow[(s + 1) % 2][:, h, :],
                                                  start=True, stop=True)
                        mm.then_inc(pv_mm, 1)
                    if f.tok:
                        tok_taps(t, u, 4 * s + 2, 1)
                    if f.proj and s == 0:
                        wait(pe, tok_evac, t)
                        wait(pe, conv_done, (t - 1) * NBLK)
                        for b in range(GB):
                            mm = nc.tensor.transpose(psP[0][:NT, b * D:(b + 1) * D], tokT[:, b * NT:(b + 1) * NT],
                                                     ident[:, :])
                        mm.then_inc(tok_tr, 1)
                    if f.proj and s == 1:
                        wait(pe, xn_ready, t)
                        for b in range(GB):
                            mm = nc.tensor.transpose(psP[1][:, b * NT:(b + 1) * NT], xn[:, b, :], ident[:NT, :NT])
                        mm.then_inc(xnT_tr, 1)
                    if f.proj:
                        for k in PROJ.get((s, 0), ()):
                            proj(t, k)
                    if f.attn and prev:
                        pe.wait_ge(v_evac, n + 1)
                    if f.scat and s == 0:
                        wait(pe, rw_done, t - 3)
                        wait(pe, a_evac, n - 1 if prev else B)
                        mm = nc.tensor.transpose(psRT, rw[:, :, :].rearrange("p b e -> p (b e)"),
                                                 ident[:NT, :NT])
                        if not prev:
                            mm.then_inc(rwT_tr, 1)
                    if prev:
                        pe.wait_ge(norm_done, n)
                        for j in range(QB):
                            mm = nc.tensor.transpose(psV[:, j * NT:(j + 1) * NT], attn[:, j * 128:(j + 1) * 128],
                                                     ident[:NT, :NT])
                        mm.then_inc(a_tr, 1)
                    if f.tok:
                        tok_taps(t, u, 4 * s + 3, 1)
                    if f.gate and s == 1:
                        wait(pe, hn_ready, t - 2)
                        for b in range(GB):
                            mm = nc.tensor.transpose(psHn[:, b * NT:(b + 1) * NT], hn[1 - u][:, b, :],
                                                     ident[:NT, :NT])
                        mm.then_inc(hnT_tr, 1)
                    if f.gate and s == 2:
                        wait(pe, hnT_evac, t - 2)
                        for b in range(GB):
                            mm = nc.tensor.matmul(psGate[:, b * E:(b + 1) * E], hnT[:, b * NT:(b + 1) * NT],
                                                  wgate[:, :], start=True, stop=True)
                        mm.then_inc(gate_mm, 1)
                    if f.gate and s == 3:
                        wait(pe, mask_done, t - 2)
                        nc.tensor.matmul(psRank[:, :], tri[:, :], mask[:, :], start=True, stop=False)
                        for b in range(GB - 1):
                            later = mask[:, b * E:(b + 1) * E].unsqueeze(1).broadcast_to([NT, GB - 1 - b, E])
                            nc.tensor.matmul(psRank[:, (b + 1) * E:].rearrange("p (b e) -> p b e", e=E), ones16[:, :NT], later,
                                             start=False, stop=(b == GB - 2))
                        for b in range(GB):
                            mm = nc.tensor.matmul(psTot, ones16[:, :], mask[:, b * E:(b + 1) * E],
                                                  start=(b == 0), stop=(b == GB - 1))
                        mm.then_inc(rank_mm, 1)
                    if f.proj:
                        for k in PROJ.get((s, 1), ()):
                            proj(t, k)
                    if prev:
                        pe.wait_ge(a_evac, n)
                        if f.gate and s == 3:
                            wait(pe, base_done, t - 2)
                        for j in range(QB):
                            mm = nc.tensor.matmul(psWout, attnT[:, j, :], wout[:, j, :],
                                                  start=(j == 0), stop=(j == QB - 1))
                        mm.then_inc(out_mm, 1)

            run(pe, step)

            pe.wait_ge(tcol_ready, 1)
            pe.wait_ge(rwT_evac, NG)
            for c in range(3):
                mm = nc.tensor.matmul(psTok[0:1, c * 128:(c + 1) * 128], tcol[:, c:c + 1], ident[:, :],
                                      start=True, stop=True)
            nc.tensor.matmul(psV[:, 0:FB * E], zeros[:, :], zeros[:, 0:FB * E], start=True, stop=False,
                             skip_group_check=True).then_inc(table_mm, 1)
            pe.wait_ge(table_ready, 1)
            pe.wait_ge(expert_w_in, 32)

            def turn(i, k, first=False):
                pe.wait_ge(xs_in[k], (i - k) * (16 // NX) + 16)
                if not first:
                    pe.wait_ge(xs_evac, i - 1)
                nc.tensor.transpose(psS[:, k % 2, 0:128], xs[k][:, :], ident[:, :]).then_inc(xs_tr, 1)

            def up(i, k, first=False):
                pe.wait_ge(xs_evac, i + 1)
                if not first:
                    pe.wait_ge(silu_done, i - 1)
                at = pe.value_load(tab[0:1, bass.ds(i + 128, 1)], min_val=0, max_val=(E - 1) * F)
                nc.tensor.matmul(psO[:, k % 2, :], xsT[k % 2][:, :], w1s[:, bass.ds(at, F)],
                                 start=True, stop=True).then_inc(up_mm, 1)

            def down(i, k):
                pe.wait_ge(silu_done, i + 1)
                at = pe.value_load(tab[0:1, bass.ds(i + 256, 1)], min_val=0, max_val=E - 1)
                for j in range(FB):
                    mm = nc.tensor.matmul(psV[:, j * E:(j + 1) * E], act[k % 2][:, j * 128:(j + 1) * 128],
                                          hotrow[:, bass.ds(at, E)], start=False, stop=True, skip_group_check=True)
                mm.then_inc(sum_mm, 1)

            turn(0, 0, True)
            turn(1, 1, True)
            up(0, 0, True)
            for i in range(1, NX):
                turn(i + 1, (i + 1) % NX)
                up(i, i, i < 2)
                down(i - 1, i - 1)
            with pe.Fori(1, NTILE // NX - 1) as r:
                for k in range(NX):
                    i = r * NX + k
                    turn(i + 1, (k + 1) % NX)
                    up(i, k)
                    down(i - 1, (k - 1) % NX)
            for i in range(NTILE - NX, NTILE):
                if i + 1 < NTILE:
                    turn(i + 1, (i + 1) % NX)
                up(i, i % NX)
                down(i - 1, (i - 1) % NX)
            down(NTILE - 1, (NTILE - 1) % NX)

            pe.wait_ge(hsum_evac, 1)
            for e in range(E):
                for j in range(FB):
                    mm = nc.tensor.matmul(psTok[:, e:e + 1], w2s[:, j, e, :], hsum[:, j * E + e:j * E + e + 1],
                                          start=(j == 0), stop=(j == FB - 1))
            mm.then_inc(down_mm, 1)
            pe.wait_ge(y_scaled, 1)
            nc.tensor.transpose(psTok[:, 128:256], yT[:, :, :].rearrange("p b e -> p (b e)"),
                                ident[:, :]).then_inc(yT_tr, 1)
            pe.wait_ge(ymix_ready, 1)

            def mix(g, u):
                pe.wait_ge(rstage_done, g + 1)
                wait(pe, out_add, g - 1)
                nc.tensor.matmul(psP[u][:NT, :], rstage[u][:, :], ymix[:, :, :].rearrange("p b d -> p (b d)"),
                                 start=True, stop=True).then_inc(mix_mm, 1)

            for g in range(2):
                mix(g, g)
            with pe.Fori(1, NG // 2) as r:
                for u in range(2):
                    mix(r * 2 + u, u)

        @block.scalar
        def _(ac):
            ac.dma_start(wtok[:, :, :], w_tok).then_inc(tok_w_in, 16)
            for dst, src in ((btok[:, :], b_tok), (ident[:, :], c_ident), (gam[:, :], gamma), (bet[:, :], beta),
                             (bias32[:, :], c_bias), (tri32[:, :], c_tri), (misc[:, :], c_misc)):
                ac.dma_start(dst, src).then_inc(small_in, 16)
            ac.wait_ge(small_in, 16 * 7)

            def tap2(t, u, k):
                wait(ac, proj_mm, (t - 1) * NBLK + (k + 1))
                if k == 0 and isinstance(t, int) and t == 1:
                    ac.wait_ge(taps_ready, 1)
                nc.scalar.activation(qkv[1 - u][:, k, :, :], psP[k % 2][:, 0:GT].rearrange("p (b n) -> p b n", n=NT),
                                     ACT.Copy, scale=taps[:, k, 2:3]).then_inc(tap2_done, 1)

            def step(t, u, f):
                for s in range(GB):
                    n = (t - 2) * GB + s
                    prev = f.attn and s > 0 or f.last and s == 0
                    if prev:
                        wait(ac, pv_mm, n - 1)
                        for a in range(2):
                            ac.wait_ge(p_tr, n * 2 - 1 + a)
                            nc.scalar.activation(probT[:, a, :, :].rearrange("p h n -> p (h n)"),
                                                 psS[:NT, a, 0:4 * NT], ACT.Copy).then_inc(p_evac, 1)
                    if f.attn:
                        ac.wait_ge(v_tr, n + 1)
                        wait(ac, pv_mm, n - 1)
                        if isinstance(t, int) and t == 2 and s == 0:
                            ac.wait_ge(vones_ready, 2)
                        nc.scalar.activation(vrow[s % 2][:, :, 0:DH],
                                             psV[:NT, :].rearrange("p (h d) -> p h d", d=DH), ACT.Copy)\
                            .then_inc(v_evac, 1)
                    if f.proj and s == 0:
                        wait(ac, tok_tr, t)
                        nc.scalar.activation(resid[:, bass.ds((t - 1) * (GB * D), GB * D)], psP[0][:NT, :],
                                             ACT.Copy).then_inc(res_evac, 1)
                    if f.proj and s == 1:
                        wait(ac, xnT_tr, t)
                        nc.scalar.activation(xnT[:, :], psP[1][:, 0:GT], ACT.Identity, bias=bet[:, 0:1],
                                             scale=gam[:, 0:1]).then_inc(xnT_evac, 1)
                    if f.proj:
                        for k in PROJ.get((s, 0), ()):
                            tap2(t, u, k)
                    if f.scat and s == 0:
                        if prev:
                            ac.wait_ge(a_tr, n)
                        else:
                            ac.wait_ge(rwT_tr, 1)
                        nc.scalar.activation(rwT[:, bass.ds((t - 4) * NT, NT)], psRT, ACT.Copy).then_inc(rwT_evac, 1)
                    if prev:
                        ac.wait_ge(a_tr, n)
                        wait(ac, out_mm, n - 1)
                        nc.scalar.activation(attnT[:, :, :].rearrange("p j n -> p (j n)"), psV[:, 0:GT],
                                             ACT.Copy).then_inc(a_evac, 1)
                    if f.attn:
                        ac.wait_ge(shift_done, n + 1)
                        flat = prob[:, :, :, :].rearrange("p a h n -> p (a h n)")
                        nc.scalar.activation(flat, flat, ACT.Exp).then_inc(exp_done, 1)
                    if f.gate and s == 1:
                        wait(ac, hnT_tr, t - 2)
                        nc.scalar.activation(hnT[:, :], psHn, ACT.Copy).then_inc(hnT_evac, 1)
                    if f.gate and s == 2:
                        wait(ac, gap_done, t - 2)
                        nc.scalar.activation(egap[:, :], gap[:, :], ACT.Exp).then_inc(egap_done, 1)
                    if f.proj:
                        for k in PROJ.get((s, 1), ()):
                            tap2(t, u, k)
                    if f.tok and s == GB - 1:
                        wait(ac, tok_mm, t + 1)
                        wait(ac, tok_tr, t)
                        nc.scalar.activation(tokT[:, :], psTok[:, 0:GT], ACT.Identity,
                                             bias=btok[:, 0:1]).then_inc(tok_evac, 1)

            run(ac, step)

            def silu(i, k, first=False):
                ac.wait_ge(up_mm, i + 1)
                if not first:
                    ac.wait_ge(sum_mm, i - 1)
                nc.scalar.activation(act[k][:, :], psO[:, k, :], ACT.Silu).then_inc(silu_done, 1)

            for i in range(2):
                silu(i, i, True)
            with ac.Fori(1, NTILE // 2) as r:
                for k in range(2):
                    silu(r * 2 + k, k)

            def stage(g, u):
                wait(ac, mix_mm, g - 1)
                nc.scalar.activation(rstage[u][:, :], rwT[:, bass.ds(g * NT, NT)], ACT.Copy).then_inc(rstage_done, 1)

            ac.wait_ge(rwT_evac, NG)
            for g in range(2):
                stage(g, g)
            with ac.Fori(1, NG // 2) as r:
                for u in range(2):
                    stage(r * 2 + u, u)

        @block.vector
        def _(dve):
            for u in range(2):
                nc.vector.memset(vrow[u][:, :, DH:DH + 1], 1.0).then_inc(vones_ready, 1)
            nc.vector.memset(zeros[:, :], 0.0).then_inc(zeros_ready, 1)
            nc.vector.memset(rw[:, :, :], 0.0).then_inc(rwzero_ready, 1)
            dve.wait_ge(small_in, 16 * 7)
            nc.vector.tensor_copy(base[0][:, :], misc[:, C_BASE:C_BASE + E]).then_inc(consts_ready, 1)
            dve.wait_ge(proj_w_in, 16 * 8)
            nc.vector.tensor_scalar(taps[:, 0:QB, :], taps[:, 0:QB, :], float(DH) ** -0.5, None,
                                    ALU.mult).then_inc(taps_ready, 1)
            dve.wait_ge(taps_ready, 1)
            dve.wait_ge(rwzero_ready, 1)
            dve.wait_ge(consts_ready, 1)

            def conv(t, u, k):
                src = psP[k % 2][:, 0:GT].rearrange("p (b n) -> p b n", n=NT)
                dst = qkv[1 - u][:, k, :, :]
                wait(dve, tap2_done, (t - 1) * NBLK + (k + 1))
                nc.vector.scalar_tensor_tensor(dst[:, :, 1:NT], src[:, :, 0:NT - 1], taps[:, k, 1:2], dst[:, :, 1:NT],
                                               ALU.mult, ALU.add).then_inc(tap1_done, 1)
                wait(dve, tap1_done, (t - 1) * NBLK + (k + 1))
                nc.vector.scalar_tensor_tensor(dst[:, :, 2:NT], src[:, :, 0:NT - 2], taps[:, k, 0:1], dst[:, :, 2:NT],
                                               ALU.mult, ALU.add).then_inc(conv_done, 1)

            def norm(g, src, stat, mv, dst, s_stat, s_mv, s_rstd, rstd, s_done):
                for b in range(GB):
                    i = nc.vector.bn_stats(stat[:, b, :], src(b))
                i.then_inc(s_stat, 1)
                wait_apart(dve, s_stat, g + 1)
                for b in range(GB):
                    i = nc.vector.bn_aggr(mv[:, b, :], stat[:, b, :])
                i.then_inc(s_mv, 1)
                wait(dve, s_rstd, g + 1)
                for b in range(GB):
                    i = nc.vector.tensor_scalar(dst[:, b, :], src(b), mv[:, b, 0:1], rstd[:, b:b + 1],
                                                ALU.subtract, ALU.mult)
                i.then_inc(s_done, 1)

            def step(t, u, f):
                for s in range(GB):
                    n = (t - 2) * GB + s
                    prev = f.attn and s > 0 or f.last and s == 0
                    if f.attn:
                        dve.wait_ge(s_mm, n + 1)
                        nc.vector.tensor_reduce(rmax[:, :, :], heads(psS, NT), AXX, ALU.max).then_inc(max_done, 1)
                        dve.wait_ge(max_done, n + 1)
                        wait(dve, p_tr, n * 2)
                        nc.vector.tensor_tensor(prob[:, :, :, :], heads(psS, NT),
                                                rmax[:, :, :].unsqueeze(3).broadcast_to([NT, 2, 4, NT]),
                                                ALU.subtract).then_inc(shift_done, 1)
                    if prev:
                        o = heads(psO, DH + 1)
                        dve.wait_ge(pv_mm, n)
                        nc.vector.reciprocal(rden[:, :, :], o[:, :, :, DH]).then_inc(den_done, 1)
                        dve.wait_ge(den_done, n)
                        wait(dve, a_tr, n - 1)
                        nc.vector.tensor_tensor(attn[:, :].rearrange("p (a h d) -> p a h d", a=2, d=DH),
                                                o[:, :, :, 0:DH],
                                                rden[:, :, :].unsqueeze(3).broadcast_to([NT, 2, 4, DH]),
                                                ALU.mult).then_inc(norm_done, 1)
                    if f.proj and s == 0:
                        wait(dve, res_evac, t)
                        norm(t - 1, lambda b: resid[:, bass.ds((t - 1) * (GB * D) + b * D, D)], stat, mv, xn,
                             ln_stat, ln_mv, ln_rstd, rstd, xn_ready)
                    if f.gate and s == 1:
                        wait(dve, res_add, (t - 2) * GB)
                        wait(dve, scattered, (t - 4) * (16 * 2 * GB))
                        norm(t - 3, lambda b: resid[:, bass.ds((t - 3) * (GB * D) + b * D, D)], stat2, mv2, hn[1 - u],
                             ln2_stat, ln2_mv, ln2_rstd, rstd2, hn_ready)
                    if f.gate and s == 2:
                        route(t - 3)
                    if f.gate and s == 3:
                        place(t - 3, u)
                    if f.proj:
                        for half_ in range(2):
                            for k in PROJ.get((s, half_), ()):
                                conv(t, u, k)
                    if prev:
                        dve.wait_ge(out_mm, n)
                        res = resid[:, bass.ds((n - 1) * D, D)]
                        nc.vector.tensor_tensor(res, psWout, res, ALU.add).then_inc(res_add, 1)

            def route(g):
                wait(dve, gate_mm, g + 1)
                nc.vector.tensor_copy(logit[:, :, :].rearrange("p b e -> p (b e)"), psGate).then_inc(logit_copy, 1)
                wait_apart(dve, logit_copy, g + 1)
                for b in range(GB):
                    i = nc.vector.max(top[:, b, :], logit[:, b, :])
                i.then_inc(top_done, 1)
                wait_apart(dve, top_done, g + 1)
                for b in range(GB):
                    i = nc.vector.max_index(topi[:, b, :], top[:, b, :], logit[:, b, :])
                i.then_inc(topi_done, 1)
                nc.vector.tensor_tensor(gap[:, :], top[:, :, 1], top[:, :, 0], ALU.subtract).then_inc(gap_done, 1)
                wait(dve, topi_done, g + 1)
                nc.vector.tensor_copy(idxf[:, :, :], topi[:, :, 0:2].rearrange("p b k -> p k b")).then_inc(idxf_done, 1)
                wait(dve, idxf_done, g + 1)
                nc.vector.tensor_tensor(hot[:, :, :], iota.unsqueeze(1).broadcast_to([NT, 2 * GB, E]),
                                        idxf[:, :, :].rearrange("p k b -> p (k b)").unsqueeze(2)
                                        .broadcast_to([NT, 2 * GB, E]), ALU.is_equal).then_inc(hot_done, 1)
                wait(dve, hot_done, g + 1)
                nc.vector.tensor_tensor(mask[:, :].rearrange("p (b e) -> p b e", e=E), hot[:, 0:GB, :],
                                        hot[:, GB:, :], ALU.add).then_inc(mask_done, 1)

            def place(g, u):
                wait(dve, egap_done, g + 1)
                nc.vector.tensor_scalar(wden[:, :], egap[:, :], 1.0, None, ALU.add).then_inc(wden_done, 1)
                wait(dve, rank_mm, g + 1)
                was = base[1 - u]
                nc.vector.tensor_tensor(pos[:, :].rearrange("p (b e) -> p b e", e=E),
                                        psRank.rearrange("p (b e) -> p b e", e=E),
                                        was[:NT, :].unsqueeze(1).broadcast_to([NT, GB, E]), ALU.add)\
                    .then_inc(pos_done, 1)
                nc.vector.tensor_tensor(base[u][:, :], was[:, :], psTot, ALU.add).then_inc(base_done, 1)
                wait(dve, wden_done, g + 1)
                nc.vector.reciprocal(wts[:, 0, :], wden[:, :]).then_inc(w0_done, 1)
                wait(dve, pos_done, g + 1)
                nc.vector.tensor_tensor(sel[:, :, :].rearrange("p (k b) e -> p k (b e)", k=2),
                                        hot[:, :, :].rearrange("p (k b) e -> p k (b e)", k=2),
                                        pos[:, :].unsqueeze(1).broadcast_to([NT, 2, GB * E]), ALU.mult)\
                    .then_inc(sel_done, 1)
                wait(dve, w0_done, g + 1)
                nc.vector.tensor_tensor(wts[:, 1, :], egap[:, :], wts[:, 0, :], ALU.mult).then_inc(w1_done, 1)
                wait(dve, sel_done, g + 1)
                nc.vector.tensor_reduce(slotf[:, :], sel[:, :, :], AXX, ALU.add).then_inc(slotf_done, 1)
                wait(dve, w1_done, g + 1)
                nc.vector.tensor_tensor(wsel[:, :, :], hot[:, :, :],
                                        wts[:, :, :].rearrange("p k b -> p (k b)").unsqueeze(2)
                                        .broadcast_to([NT, 2 * GB, E]), ALU.mult).then_inc(wsel_done, 1)
                wait(dve, slotf_done, g + 1)
                nc.vector.tensor_copy(slot[u][:, :], slotf[:, :]).then_inc(slot_done, 1)
                wait(dve, wsel_done, g + 1)
                wait(dve, rwT_evac, g)
                nc.vector.tensor_tensor(rw[:, :, 0:E], wsel[:, 0:GB, :], wsel[:, GB:, :], ALU.add).then_inc(rw_done, 1)
                wait(dve, base_done, g + 1)

            run(dve, step)

            steps = [0]

            def link(ins):
                steps[0] += 1
                ins.then_inc(dve_step, 1)
                dve.wait_ge(dve_step, steps[0])

            last = base[(NG + 2) % 2]
            nc.vector.tensor_copy(taili[:, :], last[0:1, :]).then_inc(tail_ready, 1)
            link(nc.vector.tensor_tensor(cnt[:, :], last[:, :], misc[:, C_BASE:C_BASE + E], ALU.subtract))
            link(nc.vector.tensor_scalar(cnti[:, :], cnt[:, :], 127.0, None, ALU.add))
            link(nc.vector.tensor_scalar(cntt[:, :], cnti[:, :], 7, None, ALU.arith_shift_right))
            link(nc.vector.tensor_copy(ntl[:, :], cntt[:, :]))
            link(nc.vector.memset(ones[:, :], 1.0))
            link(nc.vector.memset(yT[:, :, :], 0.0))
            link(nc.vector.tensor_tensor_scan(tend[:, :], ones[:, :], ntl[:, :], 0.0, ALU.mult, ALU.add))
            link(nc.vector.tensor_scalar(past[:, :], tend[:, :], misc[:, C_TILE:C_TILE + 1], None, ALU.is_le))
            link(nc.vector.tensor_reduce(tcol[:, 3:4], past[:, :], AXX, ALU.add))
            link(nc.vector.tensor_tensor(pastt[:, :], past[:, :], tend[:, :], ALU.mult))
            link(nc.vector.tensor_reduce(tcol[:, 4:5], pastt[:, :], AXX, ALU.max))
            link(nc.vector.tensor_scalar(tcol[:, 5:6], tcol[:, 3:4], float(E), 128.0, ALU.is_lt, ALU.mult))
            link(nc.vector.tensor_tensor(tcol[:, 6:7], misc[:, C_TILE:C_TILE + 1], tcol[:, 4:5], ALU.subtract))
            link(nc.vector.tensor_tensor(tcol[:, 6:7], tcol[:, 6:7], tcol[:, 5:6], ALU.mult))
            link(nc.vector.tensor_scalar(tcol[:, 0:1], tcol[:, 3:4], float(CAP), tcol[:, 6:7], ALU.mult, ALU.add))
            link(nc.vector.tensor_scalar(tcol[:, 1:2], tcol[:, 3:4], float(E - 1), float(F), ALU.min, ALU.mult))
            link(nc.vector.tensor_scalar(tcol[:, 2:3], tcol[:, 1:2], -1.0 / F, float(E - 1), ALU.mult, ALU.add))
            nc.vector.tensor_scalar(invc[:, :], cnt[:, :], 1.0, None, ALU.max).then_inc(tcol_ready, 1)
            dve.wait_ge(tcol_ready, 1)
            dve.wait_ge(table_mm, 1)
            link(nc.vector.reciprocal(invc[:, :], invc[:, :]))
            nc.vector.tensor_copy(tab[:, :], psTok[0:1, 0:3 * 128]).then_inc(table_ready, 1)

            def xs_copy(i, k, first=False):
                dve.wait_ge(xs_tr, i + 1)
                if not first:
                    dve.wait_ge(up_mm, i - 1)
                nc.vector.tensor_copy(xsT[k][:, :], psS[:, k, 0:128]).then_inc(xs_evac, 1)

            for i in range(2):
                xs_copy(i, i, True)
            with dve.Fori(1, NTILE // 2) as r:
                for k in range(2):
                    xs_copy(r * 2 + k, k)
            dve.wait_ge(sum_mm, NTILE)
            nc.vector.tensor_copy(hsum[:, :], psV[:, 0:FB * E]).then_inc(hsum_evac, 1)
            dve.wait_ge(down_mm, 1)
            nc.vector.tensor_tensor(yT[:, :, 0:E], psTok[:, 0:E].unsqueeze(1).broadcast_to([D, GB, E]),
                                    invc[:, :].unsqueeze(1).broadcast_to([D, GB, E]), ALU.mult).then_inc(y_scaled, 1)
            dve.wait_ge(yT_tr, 1)
            nc.vector.tensor_tensor(ymix[:, :, :], psTok[:, 128:256].unsqueeze(1).broadcast_to([128, GB, D]),
                                    misc[:, C_BLK:C_BLK + GB].unsqueeze(2).broadcast_to([128, GB, D]), ALU.mult)\
                .then_inc(ymix_ready, 1)

            def finish(g, u, first=False):
                dve.wait_ge(mix_mm, g + 1)
                if not first:
                    dve.wait_ge(out_done[u], (g - u) * 8)
                nc.vector.tensor_tensor(osb[u][:, :], psP[u][:NT, :], resid[:, bass.ds(g * (GB * D), GB * D)],
                                        ALU.add).then_inc(out_add, 1)

            for g in range(2):
                finish(g, g, True)
            with dve.Fori(1, NG // 2) as r:
                for u in range(2):
                    finish(r * 2 + u, u)

        @block.gpsimd
        def _(pool):
            pool.wait_ge(small_in, 16 * 7)
            nc.gpsimd.tensor_copy(bias[:, :, :].rearrange("p a n -> p (a n)"), bias32[:, :]).then_inc(bias_cast, 1)
            nc.gpsimd.tensor_copy(ident16[:, :], ident[:, :]).then_inc(bias_cast, 1)
            nc.gpsimd.tensor_copy(tri[:, :], tri32[:, :]).then_inc(bias_cast, 1)
            nc.gpsimd.memset(ones16[:, :], 1.0).then_inc(bias_cast, 1)
            nc.gpsimd.memset(half[:, :], -0.5).then_inc(bias_cast, 1)
            nc.gpsimd.dma_start(w1s[:, :], w1).then_inc(expert_w_in, 16)
            nc.gpsimd.dma_start(w2s[:, :, :, :], w2).then_inc(expert_w_in, 16)
            pool.wait_ge(bias_cast, 5)

            def step(t, u, f):
                if f.proj:
                    wait_apart(pool, ln_mv, t)
                    nc.gpsimd.tensor_scalar(veps[:, :], mv[:, :, 1], 1.0 + EPS, EPS * EPS, ALU.mult, ALU.add)\
                        .then_inc(ln_veps, 1)
                    wait(pool, ln_veps, t)
                    nc.gpsimd.tensor_tensor(rstd[:, :], veps[:, :], half[:, :], ALU.pow).then_inc(ln_rstd, 1)
                if f.gate:
                    wait_apart(pool, ln2_mv, t - 2)
                    nc.gpsimd.tensor_scalar(veps2[:, :], mv2[:, :, 1], 1.0, EPS, ALU.mult, ALU.add)\
                        .then_inc(ln2_veps, 1)
                    wait(pool, ln2_veps, t - 2)
                    nc.gpsimd.tensor_tensor(rstd2[:, :], veps2[:, :], half[:, :], ALU.pow).then_inc(ln2_rstd, 1)
                if f.scat:
                    scatter(t - 4, u)

            def scatter(g, u):
                wait_apart(pool, slot_done, g + 1)
                for k in range(2):
                    for b in range(GB):
                        c = k * GB + b
                        nc.gpsimd.indirect_dma_start(
                            rows, bass.IndirectOffsetOnAxis(slot[1 - u][:, c:c + 1], 0), hn[u][:, b, :], None)\
                            .then_inc(scattered, 16)

            run(pool, step)

    return nc


def kernel(**inputs):
    import numpy as np
    import concourse.bacc as bacc
    from concourse.bass_utils import run_bass_kernel_spmd

    x = np.asarray(inputs["x"])
    padded = np.zeros((B, MR * S, D), x.dtype)
    padded[:, :T] = x

    def w(name):
        return np.asarray(inputs[name])

    def blocks(a):
        return a.T.reshape(D, QB, 128)

    def tapcols(a):
        return a.reshape(QB, 128, 3).transpose(1, 0, 2)

    i, j = np.arange(NT)[:, None], np.arange(NT)[None, :]
    alibi = np.stack([np.where(j <= i, (j - i) * 0.5 ** (h + 1), -1e30) for a in range(2) for h in range(a, H, 2)], 1)
    misc = np.zeros((128, C_END), np.float32)
    misc[:, C_IOTA:C_IOTA + E] = np.arange(E)
    misc[:, C_BASE:C_BASE + E] = np.arange(E) * CAP
    misc[:, C_TILE] = np.arange(128)
    misc[:, C_BLK:C_BLK + GB] = np.arange(128)[:, None] // ESTRIDE == np.arange(GB)
    misc[:, C_HOT + E - 1] = 1.0

    data = {
        "x": padded.reshape(B, MR, S, D).transpose(3, 0, 2, 1).reshape(D, B * S * MR),
        "w_tok": w("L0_tok_W").reshape(D, D, P).transpose(1, 2, 0),
        "b_tok": w("L0_tok_b").reshape(D, 1),
        "gamma": w("L0_attn_gamma").reshape(D, 1),
        "beta": w("L0_attn_beta").reshape(D, 1),
        "wq": blocks(w("L0_attn_wq1")), "wk": blocks(w("L0_attn_wk1")), "wv": blocks(w("L0_attn_wv1")),
        "cq": tapcols(w("L0_attn_wqd")), "ck": tapcols(w("L0_attn_wkd")), "cv": tapcols(w("L0_attn_wvd")),
        "w_out": w("L0_attn_wout").T.reshape(QB, 128, D).transpose(1, 0, 2),
        "w_gate": w("L0_ffn_gate_weight").T,
        "w1": w("L0_ffn_w1").transpose(2, 0, 1).reshape(D, E * F),
        "w2": w("L0_ffn_w2").reshape(E, D, FB, 128).transpose(3, 2, 0, 1),
        "c_ident": np.eye(128, dtype=np.float32),
        "c_bias": alibi.reshape(NT, 2 * GT).astype(np.float32),
        "c_tri": (i < j).astype(np.float32),
        "c_misc": misc,
    }
    nc = bacc.Bacc("TRN2", target_bir_lowering=False, num_devices=1)
    arrays, args = {}, []
    for name, a in data.items():
        a = np.ascontiguousarray(a)
        arrays[f"in_{name}"] = a
        args.append(nc.dram_tensor(f"in_{name}", a.shape, mybir.dt.from_np(a.dtype), kind="ExternalInput").ap())
    args.append(nc.dram_tensor("out_0", (B, NT, D), F32, kind="ExternalOutput").ap())
    build(nc, *args)
    r = run_bass_kernel_spmd(nc, [arrays], core_ids=[0])
    return r.results[0]["out_0"]
```

```python
from contextlib import ExitStack

import concourse.bass as bass
from concourse import mybir

F32 = mybir.dt.float32
BF16 = mybir.dt.bfloat16
I32 = mybir.dt.int32
U32 = mybir.dt.uint32
ALU = mybir.AluOpType
ACT = mybir.ActivationFunctionType
AXX = mybir.AxisListType.X

B, T, D = 64, 750, 128
P, S = 16, 8
NT = 93
MR = NT + 1
H, DH = 8, 64
E, F = 16, 512
EPS = 1e-5
GB = 4
NG = B // GB
GT = GB * NT
QB = H * DH // 128
NBLK = 3 * QB
CAP = B * NT + 128
ROWS = E * CAP + 128
NTILE = (2 * B * NT + E * 127) // 128
FB = F // 128
ESTRIDE = 32

C_IOTA, C_BASE, C_TILE, C_BLK, C_REP, C_END = 0, E, 2 * E, 2 * E + 1, 2 * E + 1 + GB, 2 * E + 1 + GB + 128


def build(nc, x, w_tok, b_tok, gamma, beta, wq, wk, wv, cq, ck, cv, w_out, w_gate, w1, w2,
          c_ident, c_bias, c_tri, c_misc, out):
    rows = nc.dram_tensor("expert_rows", [ROWS, D], F32, kind="Internal").ap()
    ctx = ExitStack()
    with ctx:
        def sb(name, shape, dt=F32):
            return ctx.enter_context(nc.sbuf_tensor(name, shape, dt))

        def sem(name):
            return ctx.enter_context(nc.semaphore(name))

        wtok = sb("wtok", [D, P, D])
        btok = sb("btok", [D, 1])
        gam = sb("gam", [D, 1])
        bet = sb("bet", [D, 1])
        wqkv = sb("wqkv", [D, NBLK, 128])
        taps = sb("taps", [D, NBLK, 3])
        wout = sb("wout", [128, QB, D])
        wgate = sb("wgate", [D, E])
        w1s = sb("w1s", [D, E * F])
        w2keep = sb("w2keep", [128, FB // 2, E, D])
        ident = sb("ident", [128, 128])
        bias = sb("bias", [NT, 2, GT], BF16)
        ident16 = sb("ident16", [128, 128], BF16)
        tri = sb("tri", [NT, NT], BF16)
        ones16 = sb("ones16", [NT, 128], BF16)
        misc = sb("misc", [128, C_END])
        half = sb("half", [NT, GB])
        zeros = sb("zeros", [128, D])
        xbuf = [sb(f"xbuf{u}", [D, GB, S, MR]) for u in range(2)]
        tokT = sb("tokT", [D, GT])
        resid = sb("resid", [NT, B * D])
        stat = sb("stat", [NT, GB, 6])
        mv = sb("mv", [NT, GB, 2])
        veps = sb("veps", [NT, GB])
        rstd = sb("rstd", [NT, GB])
        xn = sb("xn", [NT, GB, D])
        xnT = [sb(f"xnT{u}", [D, GT]) for u in range(2)]
        qkv = [sb(f"qkv{u}", [128, NBLK, GB, NT]) for u in range(2)]
        early = qkv[1][:].rearrange("p k b n -> p (k b n)")
        bias32, tri32 = early[:NT, 0:2 * GT], early[:NT, 2 * GT:2 * GT + NT]
        vrow = [sb(f"vrow{u}", [NT, H, DH + 1]) for u in range(2)]
        rmax = sb("rmax", [NT, 2, 4])
        prob = sb("prob", [NT, 2, 4, NT])
        probT = sb("probT", [NT, 2, 4, NT])
        rden = sb("rden", [NT, 2, 4])
        attn = sb("attn", [NT, H * DH])
        attnT = sb("attnT", [128, QB, NT])
        stat2 = sb("stat2", [NT, GB, 6])
        mv2 = sb("mv2", [NT, GB, 2])
        veps2 = sb("veps2", [NT, GB])
        rstd2 = sb("rstd2", [NT, GB])
        hn = [sb(f"hn{u}", [NT, GB, D]) for u in range(2)]
        hnT = sb("hnT", [D, GT])
        logit = sb("logit", [NT, GB, E])
        top = sb("top", [NT, GB, 8])
        topi = sb("topi", [NT, GB, 8], U32)
        idxf = sb("idxf", [NT, 2, GB])
        hot = sb("hot", [NT, 2 * GB, E])
        mask = sb("mask", [NT, GB * E], BF16)
        gap = sb("gap", [NT, GB])
        egap = sb("egap", [NT, GB])
        wts = sb("wts", [NT, 2, GB])
        wden = sb("wden", [NT, GB])
        base = [sb(f"base{u}", [128, E]) for u in range(2)]
        pos = sb("pos", [NT, GB * E])
        sel = sb("sel", [NT, 2 * GB, E])
        slot = [sb(f"slot{u}", [NT, 2 * GB], I32) for u in range(2)]
        slotf = sb("slotf", [NT, 2 * GB])
        wsel = sb("wsel", [NT, 2 * GB, E])
        rw = sb("rw", [NT, GB, ESTRIDE])
        rwT = sb("rwT", [128, NG * NT])
        cnt = sb("cnt", [128, E])
        cnti = sb("cnti", [128, E], I32)
        cntt = sb("cntt", [128, E], I32)
        tcol = sb("tcol", [128, 8])
        taili = sb("taili", [1, E], I32)
        NR, NX, NO = 6, 4, 4
        AHEAD = 3
        late = [qkv[u][:].rearrange("p k b n -> p (k b n)") for u in range(2)]
        act = [late[0][:, k * F:(k + 1) * F] for k in range(NX)]
        wtile = [late[0][:, (NX + k) * F:(NX + k + 1) * F] for k in range(NX)]
        part = late[1][:, 0:NTILE * FB].rearrange("p (i j) -> p i j", j=FB)
        partT = late[1][:, 512:1024]
        ymix = late[1][:, 2 * GB * D:3 * GB * D].rearrange("p (b d) -> p b d", d=D)
        spare = late[1][:, 3 * GB * D:]
        mean = spare[:, 900:900 + FB * E * E].rearrange("p (j e) -> p j e", j=FB)
        ysb = spare[:, 1924:1924 + D]
        rstage = [spare[:, 2052 + u * NT:2052 + (u + 1) * NT] for u in range(NO)]
        osb = [sb(f"osb{u}", [NT, GB * D]) for u in range(NO)]
        flat = [xbuf[u][:].rearrange("p b r m -> p (b r m)") for u in range(2)]
        w2s = [w2keep[:, 0, :, :], w2keep[:, 1, :, :]] + [
            flat[u][:, 0:E * D].rearrange("p (e d) -> p e d", d=D) for u in range(2)]
        xs, xsT = ([flat[u][:, E * D + k * 128:E * D + (k + 1) * 128] for k in range((NR, NX)[u])] for u in range(2))
        owner = spare[:, 280:280 + E]
        tab = spare[0:1, 500:500 + 2 * 128].bitcast(I32)
        ntl, ones, tend, past, pastt, invc = (spare[:, 400 + k * E:400 + (k + 1) * E] for k in range(6))

        ps = [ctx.enter_context(nc.psum_tensor(f"ps{i}", [128, 512], F32)) for i in range(3)]
        psTok, psP = ps[0], ps[1:3]
        psS = ctx.enter_context(nc.psum_tensor("psS", [128, 2, 512], F32))
        psO = ctx.enter_context(nc.psum_tensor("psO", [128, 2, 512], F32))
        psV = ctx.enter_context(nc.psum_tensor("psV", [128, 512], F32))
        psWout = psO[:NT, 0, 384:512]
        psTot = psO[:, 0, 264:264 + E]
        psRT = psV[:, 384:384 + NT]
        psHn = psO[:, 1, 0:GT]
        psGate = psO[:NT, 1, 384:448]
        psRank = psO[:NT, 1, 448:512]

        psOut = [psP[0][:NT, :], psP[1][:NT, :], psS[:NT, 0, :], psS[:NT, 1, :]]

        psX = [psS[:, 0, :], psS[:, 1, :], psV, psTok]
        psUp = [psO[:, 0, :], psO[:, 1, :], psP[0], psP[1]]

        x_in = [sem(f"x_in{u}") for u in range(2)]
        tok_w_in, small_in, proj_w_in, expert_w_in, zero_tile_out = (
            sem("tok_w_in"), sem("small_in"), sem("proj_w_in"), sem("expert_w_in"), sem("zero_tile_out"))
        late_w_in = sem("late_w_in")
        consts_ready, zeros_ready, taps_ready, bias_cast, vones_ready, rwzero_ready = (
            sem("consts_ready"), sem("zeros_ready"), sem("taps_ready"), sem("bias_cast"),
            sem("vones_ready"), sem("rwzero_ready"))
        tok_mm, tok_evac, tok_tr, res_evac = sem("tok_mm"), sem("tok_evac"), sem("tok_tr"), sem("res_evac")
        ln_stat, ln_mv, ln_veps, ln_rstd, xn_ready = (
            sem("ln_stat"), sem("ln_mv"), sem("ln_veps"), sem("ln_rstd"), sem("xn_ready"))
        xnT_tr, xnT_evac = sem("xnT_tr"), sem("xnT_evac")
        proj_mm, tap2_done, tap1_done, conv_done = (
            sem("proj_mm"), sem("tap2_done"), sem("tap1_done"), sem("conv_done"))
        v_tr, v_evac, s_mm, max_done, shift_done, exp_done = (
            sem("v_tr"), sem("v_evac"), sem("s_mm"), sem("max_done"), sem("shift_done"), sem("exp_done"))
        p_tr, p_evac, pv_mm, den_done, norm_done = (
            sem("p_tr"), sem("p_evac"), sem("pv_mm"), sem("den_done"), sem("norm_done"))
        a_tr, a_evac, out_mm, res_add = sem("a_tr"), sem("a_evac"), sem("out_mm"), sem("res_add")
        ln2_stat, ln2_mv, ln2_veps, ln2_rstd, hn_ready = (
            sem("ln2_stat"), sem("ln2_mv"), sem("ln2_veps"), sem("ln2_rstd"), sem("hn_ready"))
        hnT_tr, hnT_evac, gate_mm, logit_copy, top_done, topi_done, idxf_done = (
            sem("hnT_tr"), sem("hnT_evac"), sem("gate_mm"), sem("logit_copy"), sem("top_done"),
            sem("topi_done"), sem("idxf_done"))
        hot_done, mask_done, gap_done, egap_done, wden_done, w0_done, w1_done = (
            sem("hot_done"), sem("mask_done"), sem("gap_done"), sem("egap_done"), sem("wden_done"),
            sem("w0_done"), sem("w1_done"))
        rank_mm, pos_done, base_done, sel_done, slotf_done, slot_done, wsel_done, rw_done = (
            sem("rank_mm"), sem("pos_done"), sem("base_done"), sem("sel_done"), sem("slotf_done"), sem("slot_done"),
            sem("wsel_done"), sem("rw_done"))
        rwT_tr, rwT_evac = sem("rwT_tr"), sem("rwT_evac")
        scattered = [sem(f"scattered{u}") for u in range(2)]
        dve_step, tcol_ready, table_mm, table_ready, tail_ready, tails_out = (
            sem("dve_step"), sem("tcol_ready"), sem("table_mm"), sem("table_ready"), sem("tail_ready"), sem("tails_out"))
        xs_in = [sem(f"xs_in{k}") for k in range(NR)]
        xs_tr, xs_evac, up_mm, silu_done, sum_mm = (
            sem("xs_tr"), sem("xs_evac"), sem("up_mm"), sem("silu_done"), sem("sum_mm"))
        w_dve_ready, w_act_ready, tile_sum, part_tr, part_evac, mean_ready, down_mm, y_evac, y_rep, ymix_ready = (
            sem("w_dve_ready"), sem("w_act_ready"), sem("tile_sum"), sem("part_tr"), sem("part_evac"), sem("mean_ready"),
            sem("down_mm"), sem("y_evac"), sem("y_rep"), sem("ymix_ready"))
        rstage_done, mix_mm, out_add = sem("rstage_done"), sem("mix_mm"), sem("out_add")
        out_done = [sem(f"out_done{u}") for u in range(NO)]

        iota = misc[:NT, C_IOTA:C_IOTA + E]

        def heads(psum, width):
            return psum[:NT, :, 0:4 * width].rearrange("p a (h c) -> p a h c", c=width)

        def wait(eng, s, value):
            if isinstance(value, int) and value <= 0:
                return
            eng.wait_ge(s, value)

        passed = sem("passed")

        def wait_apart(eng, s, value):
            wait(eng, s, value)
            if not isinstance(value, int):
                eng.sem_inc(passed, 1)

        class Stage:
            def __init__(self, on):
                self.tok, self.norm, self.proj, self.attn, self.gate, self.scat = on
                self.last = self.gate

        def stages(t):
            return Stage([0 <= t - k < NG for k in range(6)])

        FULL = Stage([True] * 6)
        LOOP_FROM, LOOP_PAIRS = 6, (NG - 6) // 2
        LAST_T = NG + 4

        def run(eng, step):
            for t in range(LOOP_FROM):
                step(t, t % 2, stages(t))
            with eng.Fori(0, LOOP_PAIRS) as r:
                for t in range(LOOP_FROM, LOOP_FROM + 2):
                    step(r * 2 + t, t % 2, FULL)
            for t in range(LOOP_FROM + 2 * LOOP_PAIRS, LAST_T + 1):
                step(t, t % 2, stages(t))


        def fetch_tiles(eng, first):
            eng.wait_ge(table_ready, 1)
            for u in range(2):
                eng.wait_ge(scattered[u], 16 * B)
            eng.wait_ge(zero_tile_out, 16)
            eng.wait_ge(tails_out, 16 * E)

            def fetch(i, k):
                start = eng.value_load(tab[0:1, bass.ds(i, 1)], min_val=0, max_val=E * CAP)
                wait(eng, xs_tr, i - (NR - 1))
                eng.dma_start(xs[k][:, :], rows[bass.ds(start, 128), :]).then_inc(xs_in[k], 16)

            for k in range(first, NR, 2):
                fetch(k, k)
            with eng.Fori(1, NTILE // NR) as r:
                for k in range(first, NR, 2):
                    fetch(r * NR + k, k)

        SHARE, ROUND = 3, 12
        copies = (lambda k: k % SHARE == SHARE - 1)

        def run_tiles(eng, body):
            for k in range(ROUND):
                body(0, k)
            with eng.Fori(1, NTILE // ROUND - 1) as r:
                for k in range(ROUND):
                    body(r, k)
            for k in range(ROUND):
                body(NTILE // ROUND - 1, k)

        def exists(i):
            return not isinstance(i, int) or i < NTILE

        def expert(eng, copy, i, k, done):
            at = eng.value_load(tab[0:1, bass.ds(i + 128, 1)], min_val=0, max_val=(E - 1) * F)
            wait_apart(eng, up_mm, i - (NX - 1))
            copy(wtile[k % NX][:, :], w1s[:, bass.ds(at, F)]).then_inc(done, 1)

        def tails(eng, first):
            for e in range(first, E, 2):
                start = eng.value_load(taili[0:1, e:e + 1], min_val=0, max_val=E * CAP)
                eng.dma_start(rows[bass.ds(start, 128), :], zeros[:, :]).then_inc(tails_out, 16)

        block = ctx.enter_context(nc.Block())

        @block.sync
        def _(sp):
            sp.dma_start(xbuf[0][:].rearrange("p b r m -> p (b r m)"), x[:, bass.ds(0, GB * S * MR)]).then_inc(x_in[0], 16)
            sp.dma_start(xbuf[1][:].rearrange("p b r m -> p (b r m)"), x[:, bass.ds(GB * S * MR, GB * S * MR)]).then_inc(x_in[1], 16)
            for dst, src in ((wqkv[:, 0:QB, :], wq), (wqkv[:, QB:2 * QB, :], wk), (wqkv[:, 2 * QB:, :], wv),
                             (taps[:, 0:QB, :], cq), (taps[:, QB:2 * QB, :], ck), (taps[:, 2 * QB:, :], cv),
                             (wout[:, :, :], w_out), (wgate[:, :], w_gate)):
                sp.dma_start(dst, src).then_inc(proj_w_in, 16)
            with sp.Fori(0, (NG - 2) // 2) as r:
                for u in range(2):
                    sp.wait_ge(tok_mm, r * 2 + (u + 1))
                    sp.dma_start(xbuf[u][:].rearrange("p b r m -> p (b r m)"),
                                 x[:, bass.ds((r * 2 + (u + 2)) * (GB * S * MR), GB * S * MR)]).then_inc(x_in[u], 16)
            sp.wait_ge(tok_mm, NG)
            for u in range(2):
                sp.dma_start(w2s[2 + u], w2[:, 2 + u, :, :]).then_inc(late_w_in, 16)
            sp.wait_ge(zeros_ready, 1)
            sp.dma_start(rows[E * CAP:ROWS, :], zeros[:, :]).then_inc(zero_tile_out, 16)
            sp.wait_ge(tail_ready, 1)
            tails(sp, 0)
            fetch_tiles(sp, 0)
            with sp.Fori(0, NG // NO) as r:
                for u in range(NO):
                    sp.wait_ge(out_add, r * NO + (u + 1))
                    sp.dma_start(out[bass.ds((r * NO + u) * GB, GB), :, :].rearrange("b t d -> t b d"),
                                 osb[u][:, :].rearrange("t (b d) -> t b d", d=D)).then_inc(out_done[u], 16)
            for u in range(NO):
                sp.wait_ge(out_done[u], 16 * (NG // NO))

        @block.tensor
        def _(pe):
            pe.wait_ge(tok_w_in, 16)
            pe.wait_ge(small_in, 16 * 7)

            def tok_taps(t, u, first, count):
                if first == 0:
                    wait(pe, x_in[u], (t - u) * 8 + 16)
                    wait(pe, tok_evac, t)
                for p in range(first, first + count):
                    r, m = p % S, p // S
                    mm = nc.tensor.matmul(psTok[:, 0:GT], wtok[:, p, :], xbuf[u][:, :, r, m:m + NT],
                                          start=(p == 0), stop=(p == P - 1))
                if first + count == P:
                    mm.then_inc(tok_mm, 1)

            def proj(t, u, f, k):
                if k == 0:
                    wait(pe, xnT_evac, t - 1)
                    if isinstance(t, int) and t == 2:
                        pe.wait_ge(proj_w_in, 16 * 8)
                if k == 1 and f.norm:
                    wait(pe, res_evac, t)
                if k == 4 and f.norm:
                    wait(pe, xnT_evac, t)
                wait(pe, conv_done, (t - 2) * NBLK + (k - 1))
                nc.tensor.matmul(psP[(k + 1) % 2][:, 0:GT], wqkv[:, k, :], xnT[u][:, :], start=True,
                                 stop=True).then_inc(proj_mm, 1)

            def step(t, u, f):
                for s in range(GB):
                    n = (t - 3) * GB + s
                    prev = f.attn and s > 0 or f.last and s == 0
                    if prev:
                        pe.wait_ge(exp_done, n)
                        for a in range(2):
                            for hh in range(4):
                                mm = nc.tensor.transpose(psS[:NT, a, hh * NT:(hh + 1) * NT], prob[:, a, hh, :],
                                                         ident[:NT, :NT])
                            mm.then_inc(p_tr, 1)
                    if f.attn:
                        if s == 0:
                            pe.wait_ge(conv_done, (t - 2) * NBLK)
                        wait(pe, a_evac, n - 1)
                        for j in range(QB):
                            mm = nc.tensor.transpose(psV[:NT, j * 128:(j + 1) * 128],
                                                     qkv[1 - u][:, 2 * QB + j, s, :], ident[:, :])
                        mm.then_inc(v_tr, 1)
                    if f.proj:
                        proj(t, u, f, 3 * s)
                    if f.norm and s == 0:
                        wait(pe, tok_evac, t)
                        wait(pe, conv_done, (t - 2) * NBLK)
                        for b in range(GB):
                            mm = nc.tensor.transpose(psP[0][:NT, b * D:(b + 1) * D], tokT[:, b * NT:(b + 1) * NT],
                                                     ident[:, :])
                        mm.then_inc(tok_tr, 1)
                    if f.norm and s == 1:
                        wait(pe, xn_ready, t)
                        wait(pe, conv_done, (t - 2) * NBLK + 3)
                        for b in range(GB):
                            mm = nc.tensor.transpose(psP[1][:, b * NT:(b + 1) * NT], xn[:, b, :], ident[:NT, :NT])
                        mm.then_inc(xnT_tr, 1)
                    if f.gate and s == 2:
                        wait(pe, hn_ready, t - 3)
                        wait(pe, norm_done, n - 1 if f.attn else B)
                        for b in range(GB):
                            mm = nc.tensor.transpose(psHn[:, b * NT:(b + 1) * NT], hn[u][:, b, :],
                                                     ident[:NT, :NT])
                        mm.then_inc(hnT_tr, 1)
                    if f.tok:
                        tok_taps(t, u, 4 * s, 1)
                    if f.attn:
                        if s == 0 and isinstance(t, int) and t == 3:
                            pe.wait_ge(bias_cast, 3)
                        wait(pe, p_evac, n * 2)
                        for a in range(2):
                            nc.tensor.matmul(psS[:NT, a, 0:4 * NT], ident16[:NT, :NT], bias[:, a, :],
                                             start=True, stop=False, skip_group_check=True)
                        for hh in range(4):
                            for a in range(2):
                                lo = 64 * a
                                mm = nc.tensor.matmul(psS[:NT, a, hh * NT:(hh + 1) * NT],
                                                      qkv[1 - u][lo:lo + 64, hh, s, :], qkv[1 - u][lo:lo + 64, QB + hh, s, :],
                                                      start=False, stop=True, skip_group_check=True)
                        mm.then_inc(s_mm, 1)
                    if prev:
                        pe.wait_ge(p_evac, n * 2)
                        pe.wait_ge(v_evac, n)
                        wait(pe, norm_done, n - 1)
                        wait(pe, res_add, n - 1)
                        if f.gate and s == 2:
                            wait(pe, hnT_evac, t - 3)
                        if f.gate and s == 3:
                            wait(pe, logit_copy, t - 3)
                        if f.scat and s == 0:
                            wait(pe, pos_done, t - 4)
                        for h in range(H):
                            mm = nc.tensor.matmul(psO[:NT, h // 4, (h % 4) * (DH + 1):(h % 4 + 1) * (DH + 1)],
                                                  probT[:, h % 2, h // 2, :], vrow[(s + 1) % 2][:, h, :],
                                                  start=True, stop=True)
                        mm.then_inc(pv_mm, 1)
                    if f.proj:
                        proj(t, u, f, 3 * s + 1)
                    if f.tok:
                        tok_taps(t, u, 4 * s + 1, 2)
                    if f.attn and prev:
                        pe.wait_ge(v_evac, n + 1)
                    if f.scat and s == 0:
                        wait(pe, rw_done, t - 4)
                        wait(pe, a_evac, n - 1 if prev else B)
                        mm = nc.tensor.transpose(psRT, rw[:, :, :].rearrange("p b e -> p (b e)"),
                                                 ident[:NT, :NT])
                        if not prev:
                            mm.then_inc(rwT_tr, 1)
                    if prev:
                        pe.wait_ge(norm_done, n)
                        for j in range(QB):
                            mm = nc.tensor.transpose(psV[:, j * NT:(j + 1) * NT], attn[:, j * 128:(j + 1) * 128],
                                                     ident[:NT, :NT])
                        mm.then_inc(a_tr, 1)
                    if f.gate and s == 2:
                        wait(pe, hnT_evac, t - 3)
                        for b in range(GB):
                            mm = nc.tensor.matmul(psGate[:, b * E:(b + 1) * E], hnT[:, b * NT:(b + 1) * NT],
                                                  wgate[:, :], start=True, stop=True)
                        mm.then_inc(gate_mm, 1)
                    if f.gate and s == 3:
                        wait(pe, mask_done, t - 3)
                        nc.tensor.matmul(psRank[:, :], tri[:, :], mask[:, :], start=True, stop=False)
                        for b in range(GB - 1):
                            later = mask[:, b * E:(b + 1) * E].unsqueeze(1).broadcast_to([NT, GB - 1 - b, E])
                            nc.tensor.matmul(psRank[:, (b + 1) * E:].rearrange("p (b e) -> p b e", e=E), ones16[:, :NT], later,
                                             start=False, stop=(b == GB - 2))
                        for b in range(GB):
                            mm = nc.tensor.matmul(psTot, ones16[:, :], mask[:, b * E:(b + 1) * E],
                                                  start=(b == 0), stop=(b == GB - 1))
                        mm.then_inc(rank_mm, 1)
                    if f.tok:
                        tok_taps(t, u, 4 * s + 3, 1)
                    if f.proj:
                        proj(t, u, f, 3 * s + 2)
                    if prev:
                        pe.wait_ge(a_evac, n)
                        if f.gate and s == 3:
                            wait(pe, base_done, t - 3)
                        for j in range(QB):
                            mm = nc.tensor.matmul(psWout, attnT[:, j, :], wout[:, j, :],
                                                  start=(j == 0), stop=(j == QB - 1))
                        mm.then_inc(out_mm, 1)

            run(pe, step)

            pe.wait_ge(tcol_ready, 1)
            pe.wait_ge(rwT_evac, NG)
            for c in range(2):
                mm = nc.tensor.matmul(psTok[0:1, c * 128:(c + 1) * 128], tcol[:, c:c + 1], ident[:, :],
                                      start=True, stop=True)
            mm.then_inc(table_mm, 1)

            def turn(r, k):
                i = r * ROUND + k
                pe.wait_ge(xs_in[k % NR], r * (16 * ROUND // NR) + (16 * (k // NR) + 16))
                wait(pe, xs_evac, i - (NX - 1))
                nc.tensor.transpose(psX[k % NX][:, 0:128], xs[k % NR][:, :], ident[:, :]).then_inc(xs_tr, 1)

            def up(r, k):
                i = r * ROUND + k
                by_act = sum(copies(q) for q in range(k + 1))
                if copies(k):
                    pe.wait_ge(w_act_ready, r * (ROUND // SHARE) + by_act)
                else:
                    pe.wait_ge(w_dve_ready, r * (ROUND - ROUND // SHARE) + (k + 1 - by_act))
                pe.wait_ge(xs_evac, i + 1)
                wait(pe, silu_done, i - (NX - 1))
                for j in range(FB):
                    mm = nc.tensor.matmul(psUp[k % NX][:, j * 128:(j + 1) * 128], wtile[k % NX][:, j * 128:(j + 1) * 128],
                                          xsT[k % NX][:, :], start=True, stop=True)
                mm.then_inc(up_mm, 1)

            def tile(r, k):
                if exists(r * ROUND + (k + AHEAD)):
                    turn(r, k + AHEAD)
                up(r, k)

            for k in range(AHEAD):
                turn(0, k)
            run_tiles(pe, tile)

            pe.wait_ge(tile_sum, NTILE)
            pe.wait_ge(xs_evac, NTILE)
            for j in range(FB):
                mm = nc.tensor.transpose(psTok[:NTILE, j * 128:(j + 1) * 128], part[:, :, j], ident[:, :])
            mm.then_inc(part_tr, 1)
            pe.wait_ge(part_evac, 1)
            for j in range(FB):
                mm = nc.tensor.matmul(psV[:, j * E:(j + 1) * E], partT[:NTILE, j * 128:(j + 1) * 128],
                                      owner[:NTILE, :], start=True, stop=True)
            mm.then_inc(sum_mm, 1)
            pe.wait_ge(mean_ready, 1)
            pe.wait_ge(expert_w_in, 32)
            pe.wait_ge(late_w_in, 32)
            for e in range(E):
                for j in range(FB):
                    mm = nc.tensor.matmul(psTok[0:E, 0:D], mean[:, j, e * E:(e + 1) * E], w2s[j][:, e, :],
                                          start=(e == 0 and j == 0), stop=(e == E - 1 and j == FB - 1))
            mm.then_inc(down_mm, 1)
            pe.wait_ge(y_evac, 1)
            nc.tensor.matmul(psTok[:, 128:256], misc[0:E, C_REP:C_REP + 128], ysb[0:E, :], start=True,
                             stop=True).then_inc(y_rep, 1)
            pe.wait_ge(ymix_ready, 1)

            def mix(g, u):
                pe.wait_ge(rstage_done, g + 1)
                wait(pe, out_add, g - (NO - 1))
                nc.tensor.matmul(psOut[u], rstage[u][:, :], ymix[:, :, :].rearrange("p b d -> p (b d)"),
                                 start=True, stop=True).then_inc(mix_mm, 1)

            for g in range(NO):
                mix(g, g)
            with pe.Fori(1, NG // NO) as r:
                for u in range(NO):
                    mix(r * NO + u, u)

        @block.scalar
        def _(ac):
            ac.dma_start(wtok[:, :, :], w_tok).then_inc(tok_w_in, 16)
            for dst, src in ((btok[:, :], b_tok), (ident[:, :], c_ident), (gam[:, :], gamma), (bet[:, :], beta),
                             (bias32[:, :], c_bias), (tri32[:, :], c_tri), (misc[:, :], c_misc)):
                ac.dma_start(dst, src).then_inc(small_in, 16)
            ac.wait_ge(small_in, 16 * 7)

            def tap2(t, u, k):
                wait(ac, proj_mm, (t - 2) * NBLK + (k + 1))
                if k == 0 and isinstance(t, int) and t == 2:
                    ac.wait_ge(taps_ready, 1)
                nc.scalar.activation(qkv[u][:, k, :, :], psP[(k + 1) % 2][:, 0:GT].rearrange("p (b n) -> p b n", n=NT),
                                     ACT.Copy, scale=taps[:, k, 2:3]).then_inc(tap2_done, 1)

            def step(t, u, f):
                for s in range(GB):
                    n = (t - 3) * GB + s
                    prev = f.attn and s > 0 or f.last and s == 0
                    if prev:
                        wait(ac, pv_mm, n - 1)
                        for a in range(2):
                            ac.wait_ge(p_tr, n * 2 - 1 + a)
                            nc.scalar.activation(probT[:, a, :, :].rearrange("p h n -> p (h n)"),
                                                 psS[:NT, a, 0:4 * NT], ACT.Copy).then_inc(p_evac, 1)
                    if f.attn:
                        ac.wait_ge(v_tr, n + 1)
                        wait(ac, pv_mm, n - 1)
                        if isinstance(t, int) and t == 3 and s == 0:
                            ac.wait_ge(vones_ready, 2)
                        nc.scalar.activation(vrow[s % 2][:, :, 0:DH],
                                             psV[:NT, :].rearrange("p (h d) -> p h d", d=DH), ACT.Copy)\
                            .then_inc(v_evac, 1)
                    if f.proj:
                        tap2(t, u, 3 * s)
                    if f.norm and s == 0:
                        wait(ac, tok_tr, t)
                        nc.scalar.activation(resid[:, bass.ds((t - 1) * (GB * D), GB * D)], psP[0][:NT, :],
                                             ACT.Copy).then_inc(res_evac, 1)
                    if f.norm and s == 1:
                        wait(ac, xnT_tr, t)
                        nc.scalar.activation(xnT[1 - u][:, :], psP[1][:, 0:GT], ACT.Identity, bias=bet[:, 0:1],
                                             scale=gam[:, 0:1]).then_inc(xnT_evac, 1)
                    if f.gate and s == 2:
                        wait(ac, hnT_tr, t - 3)
                        nc.scalar.activation(hnT[:, :], psHn, ACT.Copy).then_inc(hnT_evac, 1)
                    if f.proj:
                        tap2(t, u, 3 * s + 1)
                    if f.attn:
                        ac.wait_ge(shift_done, n + 1)
                        flat = prob[:, :, :, :].rearrange("p a h n -> p (a h n)")
                        nc.scalar.activation(flat, flat, ACT.Exp).then_inc(exp_done, 1)
                    if f.scat and s == 0:
                        if prev:
                            ac.wait_ge(a_tr, n)
                        else:
                            ac.wait_ge(rwT_tr, 1)
                        nc.scalar.activation(rwT[:, bass.ds((t - 5) * NT, NT)], psRT, ACT.Copy).then_inc(rwT_evac, 1)
                    if prev:
                        ac.wait_ge(a_tr, n)
                        wait(ac, out_mm, n - 1)
                        nc.scalar.activation(attnT[:, :, :].rearrange("p j n -> p (j n)"), psV[:, 0:GT],
                                             ACT.Copy).then_inc(a_evac, 1)
                    if f.gate and s == 3:
                        wait(ac, gap_done, t - 3)
                        nc.scalar.activation(egap[:, :], gap[:, :], ACT.Exp).then_inc(egap_done, 1)
                    if f.proj:
                        tap2(t, u, 3 * s + 2)
                    if f.tok and s == GB - 1:
                        wait(ac, tok_mm, t + 1)
                        wait(ac, tok_tr, t)
                        nc.scalar.activation(tokT[:, :], psTok[:, 0:GT], ACT.Identity,
                                             bias=btok[:, 0:1]).then_inc(tok_evac, 1)

            run(ac, step)
            ac.wait_ge(tail_ready, 1)
            tails(ac, 1)

            def silu(i, k):
                ac.wait_ge(up_mm, i + 1)
                wait(ac, tile_sum, i - (NX - 1))
                nc.scalar.activation(act[k][:, :], psUp[k][:, :], ACT.Silu).then_inc(silu_done, 1)

            def xs_copy(i, k):
                ac.wait_ge(xs_tr, i + 1)
                wait(ac, up_mm, i - (NX - 1))
                nc.scalar.activation(xsT[k][:, :], psX[k][:, 0:128], ACT.Copy).then_inc(xs_evac, 1)

            def tile(r, k):
                i = r * ROUND + k
                if exists(i + AHEAD):
                    xs_copy(i + AHEAD, (k + AHEAD) % NX)
                silu(i, k % NX)
                if exists(i + NX) and copies(k + NX):
                    expert(ac, lambda d, w: nc.scalar.activation(d, w, ACT.Copy), i + NX, k + NX, w_act_ready)

            ac.wait_ge(table_ready, 1)
            ac.wait_ge(expert_w_in, 32)
            for k in range(NX):
                if copies(k):
                    expert(ac, lambda d, w: nc.scalar.activation(d, w, ACT.Copy), k, k, w_act_ready)
            for k in range(AHEAD):
                xs_copy(k, k)
            run_tiles(ac, tile)

            def stage(g, u):
                wait(ac, mix_mm, g - (NO - 1))
                nc.scalar.activation(rstage[u][:, :], rwT[:, bass.ds(g * NT, NT)], ACT.Copy).then_inc(rstage_done, 1)

            ac.wait_ge(rwT_evac, NG)
            for g in range(NO):
                stage(g, g)
            with ac.Fori(1, NG // NO) as r:
                for u in range(NO):
                    stage(r * NO + u, u)

        @block.vector
        def _(dve):
            for u in range(2):
                nc.vector.memset(vrow[u][:, :, DH:DH + 1], 1.0).then_inc(vones_ready, 1)
            nc.vector.memset(zeros[:, :], 0.0).then_inc(zeros_ready, 1)
            nc.vector.memset(rw[:, :, :], 0.0).then_inc(rwzero_ready, 1)
            dve.wait_ge(small_in, 16 * 7)
            nc.vector.tensor_copy(base[0][:, :], misc[:, C_BASE:C_BASE + E]).then_inc(consts_ready, 1)
            dve.wait_ge(proj_w_in, 16 * 8)
            nc.vector.tensor_scalar(taps[:, 0:QB, :], taps[:, 0:QB, :], float(DH) ** -0.5, None,
                                    ALU.mult).then_inc(taps_ready, 1)
            dve.wait_ge(taps_ready, 1)
            dve.wait_ge(rwzero_ready, 1)
            dve.wait_ge(consts_ready, 1)

            def conv(t, u, k):
                src = psP[(k + 1) % 2][:, 0:GT].rearrange("p (b n) -> p b n", n=NT)
                dst = qkv[u][:, k, :, :]
                wait(dve, tap2_done, (t - 2) * NBLK + (k + 1))
                nc.vector.scalar_tensor_tensor(dst[:, :, 1:NT], src[:, :, 0:NT - 1], taps[:, k, 1:2], dst[:, :, 1:NT],
                                               ALU.mult, ALU.add).then_inc(tap1_done, 1)
                wait(dve, tap1_done, (t - 2) * NBLK + (k + 1))
                nc.vector.scalar_tensor_tensor(dst[:, :, 2:NT], src[:, :, 0:NT - 2], taps[:, k, 0:1], dst[:, :, 2:NT],
                                               ALU.mult, ALU.add).then_inc(conv_done, 1)

            def stats(g, stat, mv, s_stat, s_mv):
                for b in range(GB):
                    i = nc.vector.bn_stats(stat[:, b, :], resid[:, bass.ds(g * (GB * D) + b * D, D)])
                i.then_inc(s_stat, 1)
                wait_apart(dve, s_stat, g + 1)
                for b in range(GB):
                    i = nc.vector.bn_aggr(mv[:, b, :], stat[:, b, :])
                i.then_inc(s_mv, 1)

            def normalise(g, mv, rstd, dst, s_rstd, s_done):
                wait(dve, s_rstd, g + 1)
                for b in range(GB):
                    i = nc.vector.tensor_scalar(dst[:, b, :], resid[:, bass.ds(g * (GB * D) + b * D, D)],
                                                mv[:, b, 0:1], rstd[:, b:b + 1], ALU.subtract, ALU.mult)
                i.then_inc(s_done, 1)

            def step(t, u, f):
                for s in range(GB):
                    n = (t - 3) * GB + s
                    prev = f.attn and s > 0 or f.last and s == 0
                    if f.proj:
                        conv(t, u, 3 * s)
                    if f.scat and s == 0:
                        place(t - 5, 1 - u)
                    if f.gate and s == 1:
                        wait(dve, res_add, (t - 3) * GB)
                        stats(t - 4, stat2, mv2, ln2_stat, ln2_mv)
                    if f.gate and s == 3:
                        choose(t - 4)
                    if f.attn:
                        dve.wait_ge(s_mm, n + 1)
                        nc.vector.tensor_reduce(rmax[:, :, :], heads(psS, NT), AXX, ALU.max).then_inc(max_done, 1)
                        dve.wait_ge(max_done, n + 1)
                        wait(dve, p_tr, n * 2)
                        nc.vector.tensor_tensor(prob[:, :, :, :], heads(psS, NT),
                                                rmax[:, :, :].unsqueeze(3).broadcast_to([NT, 2, 4, NT]),
                                                ALU.subtract).then_inc(shift_done, 1)
                    if prev:
                        o = heads(psO, DH + 1)
                        dve.wait_ge(pv_mm, n)
                        nc.vector.reciprocal(rden[:, :, :], o[:, :, :, DH]).then_inc(den_done, 1)
                        dve.wait_ge(den_done, n)
                        wait(dve, a_tr, n - 1)
                        nc.vector.tensor_tensor(attn[:, :].rearrange("p (a h d) -> p a h d", a=2, d=DH),
                                                o[:, :, :, 0:DH],
                                                rden[:, :, :].unsqueeze(3).broadcast_to([NT, 2, 4, DH]),
                                                ALU.mult).then_inc(norm_done, 1)
                    if f.norm and s == 0:
                        wait(dve, res_evac, t)
                        stats(t - 1, stat, mv, ln_stat, ln_mv)
                    if f.proj:
                        conv(t, u, 3 * s + 1)
                    if f.gate and s == 1:
                        wait(dve, scattered[u], (t - u - 4) * (16 * GB))
                        normalise(t - 4, mv2, rstd2, hn[u], ln2_rstd, hn_ready)
                    if f.gate and s == 3:
                        rank(t - 4, u)
                    if f.proj:
                        conv(t, u, 3 * s + 2)
                    if f.norm and s == 0:
                        normalise(t - 1, mv, rstd, xn, ln_rstd, xn_ready)
                    if f.gate and s == 2:
                        route(t - 4)
                    if prev:
                        dve.wait_ge(out_mm, n)
                        res = resid[:, bass.ds((n - 1) * D, D)]
                        nc.vector.tensor_tensor(res, psWout, res, ALU.add).then_inc(res_add, 1)

            def route(g):
                wait(dve, gate_mm, g + 1)
                nc.vector.tensor_copy(logit[:, :, :].rearrange("p b e -> p (b e)"), psGate).then_inc(logit_copy, 1)
                wait_apart(dve, logit_copy, g + 1)
                for b in range(GB):
                    i = nc.vector.max(top[:, b, :], logit[:, b, :])
                i.then_inc(top_done, 1)
                wait_apart(dve, top_done, g + 1)
                for b in range(GB):
                    i = nc.vector.max_index(topi[:, b, :], top[:, b, :], logit[:, b, :])
                i.then_inc(topi_done, 1)
                nc.vector.tensor_tensor(gap[:, :], top[:, :, 1], top[:, :, 0], ALU.subtract).then_inc(gap_done, 1)

            def choose(g):
                wait(dve, topi_done, g + 1)
                nc.vector.tensor_copy(idxf[:, :, :], topi[:, :, 0:2].rearrange("p b k -> p k b")).then_inc(idxf_done, 1)
                wait(dve, idxf_done, g + 1)
                nc.vector.tensor_tensor(hot[:, :, :], iota.unsqueeze(1).broadcast_to([NT, 2 * GB, E]),
                                        idxf[:, :, :].rearrange("p k b -> p (k b)").unsqueeze(2)
                                        .broadcast_to([NT, 2 * GB, E]), ALU.is_equal).then_inc(hot_done, 1)
                wait(dve, hot_done, g + 1)
                nc.vector.tensor_tensor(mask[:, :].rearrange("p (b e) -> p b e", e=E), hot[:, 0:GB, :],
                                        hot[:, GB:, :], ALU.add).then_inc(mask_done, 1)

            def rank(g, u):
                wait(dve, rank_mm, g + 1)
                was = base[u]
                nc.vector.tensor_tensor(pos[:, :].rearrange("p (b e) -> p b e", e=E),
                                        psRank.rearrange("p (b e) -> p b e", e=E),
                                        was[:NT, :].unsqueeze(1).broadcast_to([NT, GB, E]), ALU.add)\
                    .then_inc(pos_done, 1)
                nc.vector.tensor_tensor(base[1 - u][:, :], was[:, :], psTot, ALU.add).then_inc(base_done, 1)

            def place(g, u):
                wait(dve, egap_done, g + 1)
                nc.vector.tensor_scalar(wden[:, :], egap[:, :], 1.0, None, ALU.add).then_inc(wden_done, 1)
                wait(dve, wden_done, g + 1)
                nc.vector.reciprocal(wts[:, 0, :], wden[:, :]).then_inc(w0_done, 1)
                wait(dve, pos_done, g + 1)
                nc.vector.tensor_tensor(sel[:, :, :].rearrange("p (k b) e -> p k (b e)", k=2),
                                        hot[:, :, :].rearrange("p (k b) e -> p k (b e)", k=2),
                                        pos[:, :].unsqueeze(1).broadcast_to([NT, 2, GB * E]), ALU.mult)\
                    .then_inc(sel_done, 1)
                wait(dve, w0_done, g + 1)
                nc.vector.tensor_tensor(wts[:, 1, :], egap[:, :], wts[:, 0, :], ALU.mult).then_inc(w1_done, 1)
                wait(dve, sel_done, g + 1)
                nc.vector.tensor_reduce(slotf[:, :], sel[:, :, :], AXX, ALU.add).then_inc(slotf_done, 1)
                wait(dve, w1_done, g + 1)
                nc.vector.tensor_tensor(wsel[:, :, :], hot[:, :, :],
                                        wts[:, :, :].rearrange("p k b -> p (k b)").unsqueeze(2)
                                        .broadcast_to([NT, 2 * GB, E]), ALU.mult).then_inc(wsel_done, 1)
                wait(dve, slotf_done, g + 1)
                nc.vector.tensor_copy(slot[u][:, :], slotf[:, :]).then_inc(slot_done, 1)
                wait(dve, wsel_done, g + 1)
                wait(dve, rwT_evac, g)
                nc.vector.tensor_tensor(rw[:, :, 0:E], wsel[:, 0:GB, :], wsel[:, GB:, :], ALU.add).then_inc(rw_done, 1)
                wait(dve, base_done, g + 1)

            run(dve, step)

            steps = [0]

            def link(ins):
                steps[0] += 1
                ins.then_inc(dve_step, 1)
                dve.wait_ge(dve_step, steps[0])

            last = base[NG % 2]
            nc.vector.tensor_copy(taili[:, :], last[0:1, :]).then_inc(tail_ready, 1)
            link(nc.vector.tensor_tensor(cnt[:, :], last[:, :], misc[:, C_BASE:C_BASE + E], ALU.subtract))
            link(nc.vector.tensor_scalar(cnti[:, :], cnt[:, :], 127.0, None, ALU.add))
            link(nc.vector.tensor_scalar(cntt[:, :], cnti[:, :], 7, None, ALU.arith_shift_right))
            link(nc.vector.tensor_copy(ntl[:, :], cntt[:, :]))
            link(nc.vector.memset(ones[:, :], 1.0))
            link(nc.vector.memset(mean[:, :, :], 0.0))
            link(nc.vector.tensor_tensor_scan(tend[:, :], ones[:, :], ntl[:, :], 0.0, ALU.mult, ALU.add))
            link(nc.vector.tensor_scalar(past[:, :], tend[:, :], misc[:, C_TILE:C_TILE + 1], None, ALU.is_le))
            link(nc.vector.tensor_reduce(tcol[:, 3:4], past[:, :], AXX, ALU.add))
            link(nc.vector.tensor_tensor(pastt[:, :], past[:, :], tend[:, :], ALU.mult))
            link(nc.vector.tensor_reduce(tcol[:, 4:5], pastt[:, :], AXX, ALU.max))
            link(nc.vector.tensor_scalar(tcol[:, 5:6], tcol[:, 3:4], float(E), 128.0, ALU.is_lt, ALU.mult))
            link(nc.vector.tensor_tensor(tcol[:, 6:7], misc[:, C_TILE:C_TILE + 1], tcol[:, 4:5], ALU.subtract))
            link(nc.vector.tensor_tensor(tcol[:, 6:7], tcol[:, 6:7], tcol[:, 5:6], ALU.mult))
            link(nc.vector.tensor_scalar(tcol[:, 0:1], tcol[:, 3:4], float(CAP), tcol[:, 6:7], ALU.mult, ALU.add))
            link(nc.vector.tensor_scalar(tcol[:, 2:3], tcol[:, 3:4], float(E - 1), None, ALU.min))
            link(nc.vector.tensor_scalar(tcol[:, 1:2], tcol[:, 2:3], float(F), None, ALU.mult))
            link(nc.vector.tensor_scalar(owner[:, :], misc[:, C_IOTA:C_IOTA + E], tcol[:, 2:3], None, ALU.is_equal))
            nc.vector.tensor_scalar(invc[:, :], cnt[:, :], 1.0, None, ALU.max).then_inc(tcol_ready, 1)
            dve.wait_ge(tcol_ready, 1)
            dve.wait_ge(table_mm, 1)
            link(nc.vector.reciprocal(invc[:, :], invc[:, :]))
            nc.vector.tensor_copy(tab[:, :], psTok[0:1, 0:2 * 128]).then_inc(table_ready, 1)

            def tile_total(i, k):
                wait_apart(dve, silu_done, i + 1)
                nc.vector.tensor_reduce(part[:, bass.ds(i, 1), :].rearrange("p i j -> p (i j)"),
                                        act[k][:, :].rearrange("p (j n) -> p j n", n=128), AXX, ALU.add)\
                    .then_inc(tile_sum, 1)

            dve.wait_ge(table_ready, 1)
            dve.wait_ge(expert_w_in, 32)
            for k in range(NX):
                if not copies(k):
                    expert(dve, nc.vector.tensor_copy, k, k, w_dve_ready)

            def tile(r, k):
                i = r * ROUND + k
                tile_total(i, k % NX)
                if exists(i + NX) and not copies(k + NX):
                    expert(dve, nc.vector.tensor_copy, i + NX, k + NX, w_dve_ready)

            run_tiles(dve, tile)
            dve.wait_ge(part_tr, 1)
            nc.vector.tensor_copy(partT[:NTILE, :], psTok[:NTILE, :]).then_inc(part_evac, 1)
            dve.wait_ge(sum_mm, 1)
            nc.vector.tensor_tensor(mean[:, :, 0:E * E:E + 1], psV[:, 0:FB * E].rearrange("p (j e) -> p j e", e=E),
                                    invc[:, :].unsqueeze(1).broadcast_to([128, FB, E]), ALU.mult)\
                .then_inc(mean_ready, 1)
            dve.wait_ge(down_mm, 1)
            nc.vector.tensor_copy(ysb[0:E, :], psTok[0:E, 0:D]).then_inc(y_evac, 1)
            dve.wait_ge(y_rep, 1)
            nc.vector.tensor_tensor(ymix[:, :, :], psTok[:, 128:256].unsqueeze(1).broadcast_to([128, GB, D]),
                                    misc[:, C_BLK:C_BLK + GB].unsqueeze(2).broadcast_to([128, GB, D]), ALU.mult)\
                .then_inc(ymix_ready, 1)

            def finish(g, u, first=False):
                dve.wait_ge(mix_mm, g + 1)
                if not first:
                    dve.wait_ge(out_done[u], (g - u) * (16 // NO))
                nc.vector.tensor_tensor(osb[u][:, :], psOut[u], resid[:, bass.ds(g * (GB * D), GB * D)],
                                        ALU.add).then_inc(out_add, 1)

            for g in range(NO):
                finish(g, g, True)
            with dve.Fori(1, NG // NO) as r:
                for u in range(NO):
                    finish(r * NO + u, u)

        @block.gpsimd
        def _(pool):
            pool.wait_ge(small_in, 16 * 7)
            nc.gpsimd.tensor_copy(bias[:, :, :].rearrange("p a n -> p (a n)"), bias32[:, :]).then_inc(bias_cast, 1)
            nc.gpsimd.tensor_copy(ident16[:, :], ident[:, :]).then_inc(bias_cast, 1)
            nc.gpsimd.tensor_copy(tri[:, :], tri32[:, :]).then_inc(bias_cast, 1)
            nc.gpsimd.memset(ones16[:, :], 1.0).then_inc(bias_cast, 1)
            nc.gpsimd.memset(half[:, :], -0.5).then_inc(bias_cast, 1)
            nc.gpsimd.dma_start(w1s[:, :], w1).then_inc(expert_w_in, 16)
            nc.gpsimd.dma_start(w2keep[:, :, :, :], w2[:, 0:2, :, :]).then_inc(expert_w_in, 16)
            pool.wait_ge(bias_cast, 5)

            def step(t, u, f):
                if f.norm:
                    wait_apart(pool, ln_mv, t)
                    nc.gpsimd.tensor_scalar(veps[:, :], mv[:, :, 1], 1.0 + EPS, EPS * EPS, ALU.mult, ALU.add)\
                        .then_inc(ln_veps, 1)
                    wait(pool, ln_veps, t)
                    nc.gpsimd.tensor_tensor(rstd[:, :], veps[:, :], half[:, :], ALU.pow).then_inc(ln_rstd, 1)
                if f.gate:
                    wait_apart(pool, ln2_mv, t - 3)
                    nc.gpsimd.tensor_scalar(veps2[:, :], mv2[:, :, 1], 1.0, EPS, ALU.mult, ALU.add)\
                        .then_inc(ln2_veps, 1)
                    wait(pool, ln2_veps, t - 3)
                    nc.gpsimd.tensor_tensor(rstd2[:, :], veps2[:, :], half[:, :], ALU.pow).then_inc(ln2_rstd, 1)
                if f.scat:
                    scatter(t - 5, u)

            def scatter(g, u):
                wait_apart(pool, slot_done, g + 1)
                for k in range(2):
                    for b in range(GB):
                        c = k * GB + b
                        nc.gpsimd.indirect_dma_start(
                            rows, bass.IndirectOffsetOnAxis(slot[1 - u][:, c:c + 1], 0), hn[1 - u][:, b, :], None)\
                            .then_inc(scattered[1 - u], 16)

            run(pool, step)
            fetch_tiles(pool, 1)

    return nc


def kernel(**inputs):
    import numpy as np
    import concourse.bacc as bacc
    from concourse.bass_utils import run_bass_kernel_spmd

    x = np.asarray(inputs["x"])
    padded = np.zeros((B, MR * S, D), x.dtype)
    padded[:, :T] = x

    def w(name):
        return np.asarray(inputs[name])

    def blocks(a):
        return a.T.reshape(D, QB, 128)

    def tapcols(a):
        return a.reshape(QB, 128, 3).transpose(1, 0, 2)

    i, j = np.arange(NT)[:, None], np.arange(NT)[None, :]
    alibi = np.stack([np.where(j <= i, (j - i) * 0.5 ** (h + 1), -1e30) for a in range(2) for h in range(a, H, 2)], 1)
    misc = np.zeros((128, C_END), np.float32)
    misc[:, C_IOTA:C_IOTA + E] = np.arange(E)
    misc[:, C_BASE:C_BASE + E] = np.arange(E) * CAP
    misc[:, C_TILE] = np.arange(128)
    misc[:, C_BLK:C_BLK + GB] = np.arange(128)[:, None] // ESTRIDE == np.arange(GB)
    misc[:E, C_REP:C_REP + 128] = np.arange(128)[None, :] % ESTRIDE == np.arange(E)[:, None]

    data = {
        "x": padded.reshape(B, MR, S, D).transpose(3, 0, 2, 1).reshape(D, B * S * MR),
        "w_tok": w("L0_tok_W").reshape(D, D, P).transpose(1, 2, 0),
        "b_tok": w("L0_tok_b").reshape(D, 1),
        "gamma": w("L0_attn_gamma").reshape(D, 1),
        "beta": w("L0_attn_beta").reshape(D, 1),
        "wq": blocks(w("L0_attn_wq1")), "wk": blocks(w("L0_attn_wk1")), "wv": blocks(w("L0_attn_wv1")),
        "cq": tapcols(w("L0_attn_wqd")), "ck": tapcols(w("L0_attn_wkd")), "cv": tapcols(w("L0_attn_wvd")),
        "w_out": w("L0_attn_wout").T.reshape(QB, 128, D).transpose(1, 0, 2),
        "w_gate": w("L0_ffn_gate_weight").T,
        "w1": w("L0_ffn_w1").transpose(2, 0, 1).reshape(D, E * F),
        "w2": w("L0_ffn_w2").reshape(E, D, FB, 128).transpose(3, 2, 0, 1),
        "c_ident": np.eye(128, dtype=np.float32),
        "c_bias": alibi.reshape(NT, 2 * GT).astype(np.float32),
        "c_tri": (i < j).astype(np.float32),
        "c_misc": misc,
    }
    nc = bacc.Bacc("TRN2", target_bir_lowering=False, num_devices=1)
    arrays, args = {}, []
    for name, a in data.items():
        a = np.ascontiguousarray(a)
        arrays[f"in_{name}"] = a
        args.append(nc.dram_tensor(f"in_{name}", a.shape, mybir.dt.from_np(a.dtype), kind="ExternalInput").ap())
    args.append(nc.dram_tensor("out_0", (B, NT, D), F32, kind="ExternalOutput").ap())
    build(nc, *args)
    r = run_bass_kernel_spmd(nc, [arrays], core_ids=[0])
    return r.results[0]["out_0"]
```

```python
from contextlib import ExitStack

import concourse.bass as bass
from concourse import mybir

F32 = mybir.dt.float32
F32R = mybir.dt.float32r
BF16 = mybir.dt.bfloat16
I32 = mybir.dt.int32
U32 = mybir.dt.uint32
ALU = mybir.AluOpType
ACT = mybir.ActivationFunctionType
AXX = mybir.AxisListType.X

B, T, D = 64, 750, 128
P, S = 16, 8
NT = 93
MR = NT + 1
H, DH = 8, 64
E, F = 16, 512
EPS = 1e-5
GB = 4
NG = B // GB
GM = GB * MR
PIECE = 2 * GM
NPIECE = NG * GB
GT = GB * NT
QB = H * DH // 128
NBLK = 3 * QB
CAP = B * NT + 128
ROWS = E * CAP + 128
NTILE = (2 * B * NT + E * 127) // 128
FB = F // 128
W1P = E * F // (2 * GB)
ESTRIDE = 32

C_IOTA, C_BASE, C_TILE, C_BLK, C_REP, C_END = 0, E, 2 * E, 2 * E + 1, 2 * E + 1 + GB, 2 * E + 1 + GB + 128


def build(nc, x, w_tok, b_tok, gamma, beta, wq, wk, wv, cq, ck, cv, w_out, w_gate, w1, w2,
          c_ident, c_bias, c_tri, c_misc, out):
    rows = nc.dram_tensor("expert_rows", [ROWS, D], F32, kind="Internal").ap()
    ctx = ExitStack()
    with ctx:
        def sb(name, shape, dt=F32):
            return ctx.enter_context(nc.sbuf_tensor(name, shape, dt))

        def sem(name):
            return ctx.enter_context(nc.semaphore(name))

        btok = sb("btok", [D, 1])
        gam = sb("gam", [D, 1])
        bet = sb("bet", [D, 1])
        taps = sb("taps", [D, NBLK, 3])
        wout = sb("wout", [128, QB, D])
        wgate = sb("wgate", [D, E])
        w1s = sb("w1s", [D, E * F])
        ident = sb("ident", [128, 128])
        bias = sb("bias", [NT, 2, GT], BF16)
        ident16 = sb("ident16", [128, 128], BF16)
        tri = sb("tri", [NT, NT], BF16)
        ones16 = sb("ones16", [NT, 128], BF16)
        misc = sb("misc", [128, C_END])
        half = sb("half", [NT, GB])
        zeros = sb("zeros", [128, D])
        tokT = sb("tokT", [D, GT])
        resid = sb("resid", [NT, B * D])
        stat = sb("stat", [NT, GB, 6])
        mv = sb("mv", [NT, GB, 2])
        veps = sb("veps", [NT, GB])
        rstd = sb("rstd", [NT, GB])
        nmean = sb("nmean", [NT, GB])
        shift = sb("shift", [NT, GB])
        xn = sb("xn", [NT, GB, D])
        xnT = sb("xnT", [D, GT])
        qkv = [sb(f"qkv{u}", [128, NBLK, GB, NT]) for u in range(2)]
        early = qkv[1][:].rearrange("p k b n -> p (k b n)")
        bias32, tri32 = early[:NT, 0:2 * GT], early[:NT, 2 * GT:2 * GT + NT]
        early0 = qkv[0][:].rearrange("p k b n -> p (k b n)")
        wtok_raw = early0[:, 0:P * D].rearrange("p (s j e) -> p s j e", s=GB, j=4)
        wqkv_raw = early0[:, P * D:P * D + NBLK * 128].rearrange("p (k c) -> p k c", c=128)
        vrow = [sb(f"vrow{u}", [NT, H, DH + 1]) for u in range(2)]
        rmax = sb("rmax", [NT, 2, 4])
        prob = sb("prob", [NT, 2, 4, NT])
        probT = sb("probT", [NT, 2, 4, NT])
        rden = sb("rden", [NT, 2, 4])
        attn = sb("attn", [NT, H * DH])
        attnT = sb("attnT", [128, QB, NT])
        stat2 = sb("stat2", [NT, GB, 6])
        mv2 = sb("mv2", [NT, GB, 2])
        veps2 = sb("veps2", [NT, GB])
        rstd2 = sb("rstd2", [NT, GB])
        nmean2 = sb("nmean2", [NT, GB])
        shift2 = sb("shift2", [NT, GB])
        hn = [sb(f"hn{u}", [NT, GB, D]) for u in range(2)]
        hnT = sb("hnT", [D, GT])
        logit = sb("logit", [NT, GB, E])
        top = sb("top", [NT, GB, 8])
        topi = sb("topi", [NT, GB, 8], U32)
        idxf = sb("idxf", [NT, 2, GB])
        hot = sb("hot", [NT, 2 * GB, E])
        mask = sb("mask", [NT, GB * E], BF16)
        gap = sb("gap", [NT, GB])
        egap = sb("egap", [NT, GB])
        wts = sb("wts", [NT, 2, GB])
        wden = sb("wden", [NT, GB])
        base = [sb(f"base{u}", [128, E]) for u in range(2)]
        pos = sb("pos", [NT, GB * E])
        sel = sb("sel", [NT, 2 * GB, E])
        slot = [sb(f"slot{u}", [NT, 2 * GB], I32) for u in range(2)]
        slotf = sb("slotf", [NT, 2 * GB])
        wsel = sb("wsel", [NT, 2 * GB, E])
        rw = sb("rw", [NT, GB, ESTRIDE])
        rwT = sb("rwT", [128, NG * NT])
        cnt = sb("cnt", [128, E])
        cnti = sb("cnti", [128, E], I32)
        cntt = sb("cntt", [128, E], I32)
        tcol = sb("tcol", [128, 8])
        taili = sb("taili", [1, E], I32)
        NR, NX, NO = 6, 4, 4
        AHEAD = 3
        late = [qkv[u][:].rearrange("p k b n -> p (k b n)") for u in range(2)]
        act = [late[0][:, k * F:(k + 1) * F] for k in range(NX)]
        wtile = [late[0][:, (NX + k) * F:(NX + k + 1) * F] for k in range(NX)]
        part = late[1][:, 0:NTILE * FB].rearrange("p (i j) -> p i j", j=FB)
        partT = late[1][:, 512:1024]
        ymix = late[1][:, 2 * GB * D:3 * GB * D].rearrange("p (b d) -> p b d", d=D)
        spare = late[1][:, 3 * GB * D:]
        mean = spare[:, 900:900 + FB * E * E].rearrange("p (j e) -> p j e", j=FB)
        ysb = spare[:, 1924:1924 + D]
        rstage = [spare[:, 2052 + u * NT:2052 + (u + 1) * NT] for u in range(NO)]
        osb = [sb(f"osb{u}", [NT, GB * D]) for u in range(NO)]

        with ExitStack() as phase1:
            def split_sb(name, shape):
                return tuple(phase1.enter_context(nc.sbuf_tensor(f"{name}_{part}", shape, F32R)) for part in ("hi", "lo"))

            x_hi, x_lo = zip(*(split_sb(f"x{u}", [D, PIECE + 2]) for u in range(2)))
            x_raw = [phase1.enter_context(nc.sbuf_tensor(f"x_raw{u}", [D, PIECE], F32)) for u in range(2)]
            wtok_hi, wtok_lo = split_sb("wtok", [D, GB, 4, D])
            wqkv_hi, wqkv_lo = split_sb("wqkv", [D, NBLK, 128])
            xnT_hi, xnT_lo = zip(*(split_sb(f"xnT{u}", [D, GT]) for u in range(2)))
        w2s = [sb(f"w2_{j}", [128, E, D]) for j in range(FB)]
        xs = [sb(f"xs{k}", [128, D]) for k in range(NR)]
        xsT = [sb(f"xsT{k}", [D, 128]) for k in range(NX)]
        E_DVE = 8
        acc = (xs + xsT)[:E_DVE]
        unit = spare[:, 2424:2424 + E * E]
        owner = spare[:, 280:280 + E]
        tab = spare[0:1, 500:500 + 2 * 128].bitcast(I32)
        ntl, ones, tend, past, pastt, invc = (spare[:, 400 + k * E:400 + (k + 1) * E] for k in range(6))

        ps = [ctx.enter_context(nc.psum_tensor(f"ps{i}", [128, 512], F32)) for i in range(3)]
        psTok, psP = ps[0], ps[1:3]
        psS = ctx.enter_context(nc.psum_tensor("psS", [128, 2, 512], F32))
        psO = ctx.enter_context(nc.psum_tensor("psO", [128, 2, 512], F32))
        psV = ctx.enter_context(nc.psum_tensor("psV", [128, 512], F32))
        psWout = psO[:NT, 0, 384:512]
        psTot = psO[:, 0, 264:264 + E]
        psRT = psV[:, 384:384 + NT]
        psHn = psO[:, 1, 0:GT]
        psGate = psO[:NT, 1, 384:448]
        psRank = psO[:NT, 1, 448:512]

        psOut = [psP[0][:NT, :], psP[1][:NT, :], psS[:NT, 0, :], psS[:NT, 1, :]]

        psX = [psS[:, 0, :], psS[:, 1, :], psV, psTok]
        psUp = [psO[:, 0, :], psO[:, 1, :], psP[0], psP[1]]

        x_in = [sem(f"x_in{u}") for u in range(2)]
        small_in, proj_w_in, expert_w_in, zero_tile_out = (
            sem("small_in"), sem("proj_w_in"), sem("expert_w_in"), sem("zero_tile_out"))
        tok_w_in = [sem(f"tok_w_in{s}") for s in range(GB)]
        late_w_in = sem("late_w_in")
        wtok_hi_done, wtok_lo_done, wqkv_hi_done, wqkv_lo_done, pads_ready = (
            sem("wtok_hi_done"), sem("wtok_lo_done"), sem("wqkv_hi_done"), sem("wqkv_lo_done"), sem("pads_ready"))
        half_ready = sem("half_ready")
        consts_ready, zeros_ready, taps_ready, bias_cast, vones_ready, rwzero_ready = (
            sem("consts_ready"), sem("zeros_ready"), sem("taps_ready"), sem("bias_cast"),
            sem("vones_ready"), sem("rwzero_ready"))
        x_hi_done, x_lo_done = sem("x_hi_done"), sem("x_lo_done")
        tap_mm, tok_evac, tok_tr, res_evac = sem("tap_mm"), sem("tok_evac"), sem("tok_tr"), sem("res_evac")
        ln_stat, ln_mv, ln_veps, ln_nmean, ln_rstd, ln_shift, xn_ready = (
            sem("ln_stat"), sem("ln_mv"), sem("ln_veps"), sem("ln_nmean"), sem("ln_rstd"), sem("ln_shift"), sem("xn_ready"))
        xnT_tr, xnT_evac, xnT_hi_done, xnT_lo_done = (
            sem("xnT_tr"), sem("xnT_evac"), sem("xnT_hi_done"), sem("xnT_lo_done"))
        proj_mm, tap2_done, tap1_done, conv_done = (
            sem("proj_mm"), sem("tap2_done"), sem("tap1_done"), sem("conv_done"))
        v_tr, v_evac, s_mm, max_done, shift_done, exp_done = (
            sem("v_tr"), sem("v_evac"), sem("s_mm"), sem("max_done"), sem("shift_done"), sem("exp_done"))
        p_tr, p_evac, pv_mm, den_done, norm_done = (
            sem("p_tr"), sem("p_evac"), sem("pv_mm"), sem("den_done"), sem("norm_done"))
        a_tr, a_evac, out_mm, res_add = sem("a_tr"), sem("a_evac"), sem("out_mm"), sem("res_add")
        ln2_stat, ln2_mv, ln2_veps, ln2_nmean, ln2_rstd, ln2_shift, hn_ready = (
            sem("ln2_stat"), sem("ln2_mv"), sem("ln2_veps"), sem("ln2_nmean"), sem("ln2_rstd"), sem("ln2_shift"),
            sem("hn_ready"))
        hnT_tr, hnT_evac, gate_mm, logit_copy, top_done, topi_done, idxf_done = (
            sem("hnT_tr"), sem("hnT_evac"), sem("gate_mm"), sem("logit_copy"), sem("top_done"),
            sem("topi_done"), sem("idxf_done"))
        hot_done, mask_done, gap_done, egap_done, wden_done, w0_done, w1_done = (
            sem("hot_done"), sem("mask_done"), sem("gap_done"), sem("egap_done"), sem("wden_done"),
            sem("w0_done"), sem("w1_done"))
        rank_mm, pos_done, base_done, sel_done, slotf_done, slot_done, wsel_done, rw_done = (
            sem("rank_mm"), sem("pos_done"), sem("base_done"), sem("sel_done"), sem("slotf_done"), sem("slot_done"),
            sem("wsel_done"), sem("rw_done"))
        rwT_tr, rwT_evac = sem("rwT_tr"), sem("rwT_evac")
        scattered = [sem(f"scattered{u}") for u in range(2)]
        dve_step, tcol_ready, table_mm, table_ready, tail_ready, tails_out = (
            sem("dve_step"), sem("tcol_ready"), sem("table_mm"), sem("table_ready"), sem("tail_ready"), sem("tails_out"))
        xs_in = [sem(f"xs_in{k}") for k in range(NR)]
        xs_tr, xs_evac, up_mm, silu_done, sum_mm = (
            sem("xs_tr"), sem("xs_evac"), sem("up_mm"), sem("silu_done"), sem("sum_mm"))
        w_dve_ready, w_act_ready, tile_sum, part_tr, part_evac, mean_ready, down_mm, y_evac, y_rep, ymix_ready = (
            sem("w_dve_ready"), sem("w_act_ready"), sem("tile_sum"), sem("part_tr"), sem("part_evac"), sem("mean_ready"),
            sem("down_mm"), sem("y_evac"), sem("y_rep"), sem("ymix_ready"))
        unit_zero, unit_ready, acc_done = sem("unit_zero"), sem("unit_ready"), sem("acc_done")
        rstage_done, mix_mm, out_add = sem("rstage_done"), sem("mix_mm"), sem("out_add")
        out_done = [sem(f"out_done{u}") for u in range(NO)]

        iota = misc[:NT, C_IOTA:C_IOTA + E]

        def heads(psum, width):
            return psum[:NT, :, 0:4 * width].rearrange("p a (h c) -> p a h c", c=width)

        def wait(eng, s, value):
            if isinstance(value, int) and value <= 0:
                return
            eng.wait_ge(s, value)

        passed = sem("passed")

        def wait_apart(eng, s, value):
            wait(eng, s, value)
            if not isinstance(value, int):
                eng.sem_inc(passed, 1)

        class Stage:
            def more(self, t, s):
                return not isinstance(t, int) or t * GB + s + 1 < NPIECE

            def __init__(self, on):
                self.tok, self.norm, self.proj, self.attn, self.gate, self.scat = on
                self.last = self.gate

        def stages(t):
            return Stage([0 <= t - k < NG for k in range(6)])

        FULL = Stage([True] * 6)
        LOOP_FROM, LOOP_PAIRS = 6, (NG - 8) // 2
        LAST_T = NG + 4

        def run(eng, step):
            for t in range(LOOP_FROM):
                step(t, t % 2, stages(t))
            with eng.Fori(0, LOOP_PAIRS) as r:
                for t in range(LOOP_FROM, LOOP_FROM + 2):
                    step(r * 2 + t, t % 2, FULL)
            for t in range(LOOP_FROM + 2 * LOOP_PAIRS, LAST_T + 1):
                step(t, t % 2, stages(t))


        def fetch_tiles(eng, first):
            eng.wait_ge(table_ready, 1)
            for u in range(2):
                eng.wait_ge(scattered[u], 16 * B)
            eng.wait_ge(zero_tile_out, 16)
            eng.wait_ge(tails_out, 16 * E)

            def fetch(i, k):
                start = eng.value_load(tab[0:1, bass.ds(i, 1)], min_val=0, max_val=E * CAP)
                wait(eng, xs_tr, i - (NR - 1))
                eng.dma_start(xs[k][:, :], rows[bass.ds(start, 128), :]).then_inc(xs_in[k], 16)

            for k in range(first, NR, 2):
                fetch(k, k)
            with eng.Fori(1, NTILE // NR) as r:
                for k in range(first, NR, 2):
                    fetch(r * NR + k, k)

        ROUND = 12
        BY_ACT = (1, 3, 6, 8, 11)

        def copies(k):
            return k % ROUND in BY_ACT

        def run_tiles(eng, body):
            for k in range(ROUND):
                body(0, k)
            with eng.Fori(1, NTILE // ROUND - 1) as r:
                for k in range(ROUND):
                    body(r, k)
            for k in range(ROUND):
                body(NTILE // ROUND - 1, k)

        def exists(i):
            return not isinstance(i, int) or i < NTILE

        def expert(eng, copy, i, k, done):
            at = eng.value_load(tab[0:1, bass.ds(i + 128, 1)], min_val=0, max_val=(E - 1) * F)
            wait_apart(eng, up_mm, i - (NX - 1))
            copy(wtile[k % NX][:, :], w1s[:, bass.ds(at, F)]).then_inc(done, 1)

        def tails(eng, first):
            for e in range(first, E, 2):
                start = eng.value_load(taili[0:1, e:e + 1], min_val=0, max_val=E * CAP)
                eng.dma_start(rows[bass.ds(start, 128), :], zeros[:, :]).then_inc(tails_out, 16)

        block = ctx.enter_context(nc.Block())

        @block.sync
        def _(sp):
            def load(q, u):
                sp.dma_start(x_raw[u][:, :], x[:, bass.ds(q * PIECE, PIECE)]).then_inc(x_in[u], 16)

            for u in range(2):
                load(u, u)
            for dst, src in ((btok[:, :], b_tok), (ident[:, :], c_ident), (gam[:, :], gamma), (bet[:, :], beta),
                             (bias32[:, :], c_bias), (tri32[:, :], c_tri), (misc[:, :], c_misc)):
                sp.dma_start(dst, src).then_inc(small_in, 16)
            for dst, src in ((wqkv_raw[:, 0:QB, :], wq), (wqkv_raw[:, QB:2 * QB, :], wk), (wqkv_raw[:, 2 * QB:, :], wv),
                             (taps[:, 0:QB, :], cq), (taps[:, QB:2 * QB, :], ck), (taps[:, 2 * QB:, :], cv),
                             (wout[:, :, :], w_out), (wgate[:, :], w_gate)):
                sp.dma_start(dst, src).then_inc(proj_w_in, 16)
            with sp.Fori(0, NPIECE // 2 - 1) as r:
                for u in range(2):
                    sp.wait_ge(x_lo_done, r * 2 + (u + 1))
                    load(r * 2 + (u + 2), u)
            sp.wait_ge(tap_mm, NPIECE)
            for j in range(FB):
                sp.dma_start(w2s[j][:, :, :], w2[:, j, :, :]).then_inc(late_w_in, 16)
            sp.wait_ge(zeros_ready, 1)
            sp.dma_start(rows[E * CAP:ROWS, :], zeros[:, :]).then_inc(zero_tile_out, 16)
            sp.wait_ge(tail_ready, 1)
            tails(sp, 0)
            fetch_tiles(sp, 0)
            with sp.Fori(0, NG // NO) as r:
                for u in range(NO):
                    sp.wait_ge(out_add, r * NO + (u + 1))
                    sp.dma_start(out[bass.ds((r * NO + u) * GB, GB), :, :].rearrange("b t d -> t b d"),
                                 osb[u][:, :].rearrange("t (b d) -> t b d", d=D)).then_inc(out_done[u], 16)
            for u in range(NO):
                sp.wait_ge(out_done[u], 16 * (NG // NO))

        @block.tensor
        def _(pe):
            def split_product(dst, w_hi, w_lo, x_hi, x_lo, start, stop):
                nc.tensor.matmul(dst, w_hi, x_hi, start=start, stop=False)
                nc.tensor.matmul(dst, w_hi, x_lo, start=False, stop=False)
                return nc.tensor.matmul(dst, w_lo, x_hi, start=False, stop=stop)

            def tok_taps(t, s, first, count):
                if first == 0:
                    pe.wait_ge(x_lo_done, t * GB + (s + 1))
                    if isinstance(t, int) and t == 0:
                        pe.wait_ge(wtok_lo_done, s + 1)
                        pe.wait_ge(pads_ready, 4)
                    if s == 0:
                        wait(pe, tok_evac, t)
                for j in range(first, first + count):
                    at = (j // 2) * GM + j % 2
                    mm = split_product(psTok[:, 0:GM], wtok_hi[:, s, j, :], wtok_lo[:, s, j, :],
                                       x_hi[s % 2][:, at:at + GM], x_lo[s % 2][:, at:at + GM],
                                       start=(s == 0 and j == 0), stop=(s == GB - 1 and j == 3))
                if first + count == 4:
                    mm.then_inc(tap_mm, 1)

            def proj(t, u, f, k):
                if k == 0:
                    wait(pe, xnT_lo_done, t - 1)
                    if isinstance(t, int) and t == 2:
                        pe.wait_ge(wqkv_lo_done, 1)
                        pe.wait_ge(proj_w_in, 16 * 8)
                if k == 1 and f.norm:
                    wait(pe, res_evac, t)
                if k == 10 and f.norm:
                    wait(pe, xnT_evac, t)
                wait(pe, conv_done, (t - 2) * NBLK + (k - 1))
                split_product(psP[(k + 1) % 2][:, 0:GT], wqkv_hi[:, k, :], wqkv_lo[:, k, :], xnT_hi[u][:, :], xnT_lo[u][:, :],
                              start=True, stop=True).then_inc(proj_mm, 1)

            def step(t, u, f):
                for s in range(GB):
                    n = (t - 3) * GB + s
                    prev = f.attn and s > 0 or f.last and s == 0
                    if prev:
                        pe.wait_ge(exp_done, n)
                        for a in range(2):
                            for hh in range(4):
                                mm = nc.tensor.transpose(psS[:NT, a, hh * NT:(hh + 1) * NT], prob[:, a, hh, :],
                                                         ident[:NT, :NT])
                            mm.then_inc(p_tr, 1)
                    if f.gate and s == 2:
                        wait(pe, hn_ready, t - 3)
                        wait(pe, norm_done, n - 1 if f.attn else B)
                        for b in range(GB):
                            mm = nc.tensor.transpose(psHn[:, b * NT:(b + 1) * NT], hn[u][:, b, :],
                                                     ident[:NT, :NT])
                        mm.then_inc(hnT_tr, 1)
                    if f.proj and s == 0:
                        proj(t, u, f, 3 * s)
                    if f.attn:
                        if s == 0:
                            pe.wait_ge(conv_done, (t - 2) * NBLK)
                        wait(pe, a_evac, n - 1)
                        for j in range(QB):
                            mm = nc.tensor.transpose(psV[:NT, j * 128:(j + 1) * 128],
                                                     qkv[1 - u][:, 2 * QB + j, s, :], ident[:, :])
                        mm.then_inc(v_tr, 1)
                    if f.proj and s > 0:
                        proj(t, u, f, 3 * s)
                    if f.norm and s == 0:
                        wait(pe, tok_evac, t)
                        if isinstance(t, int) and t == 1:
                            pe.wait_ge(small_in, 16 * 7)
                        wait(pe, conv_done, (t - 2) * NBLK)
                        for b in range(GB):
                            mm = nc.tensor.transpose(psP[0][:NT, b * D:(b + 1) * D], tokT[:, b * NT:(b + 1) * NT],
                                                     ident[:, :])
                        mm.then_inc(tok_tr, 1)
                    if f.tok:
                        tok_taps(t, s, 0, 1)
                    if prev:
                        pe.wait_ge(p_evac, n * 2)
                        pe.wait_ge(v_evac, n)
                        wait(pe, norm_done, n - 1)
                        wait(pe, res_add, n - 1)
                        if f.gate and s == 2:
                            wait(pe, hnT_evac, t - 3)
                        if f.gate and s == 3:
                            wait(pe, logit_copy, t - 3)
                        if f.scat and s == 0:
                            wait(pe, pos_done, t - 4)
                        for h in range(H):
                            mm = nc.tensor.matmul(psO[:NT, h // 4, (h % 4) * (DH + 1):(h % 4 + 1) * (DH + 1)],
                                                  probT[:, h % 2, h // 2, :], vrow[(s + 1) % 2][:, h, :],
                                                  start=True, stop=True)
                        mm.then_inc(pv_mm, 1)
                    if f.norm and s == 3:
                        wait(pe, xn_ready, t)
                        wait(pe, conv_done, (t - 2) * NBLK + 9)
                        for b in range(GB):
                            mm = nc.tensor.transpose(psP[1][:, b * NT:(b + 1) * NT], xn[:, b, :], ident[:NT, :NT])
                        mm.then_inc(xnT_tr, 1)
                    if f.attn:
                        if s == 0 and isinstance(t, int) and t == 3:
                            pe.wait_ge(bias_cast, 4)
                        wait(pe, p_evac, n * 2)
                        for a in range(2):
                            nc.tensor.matmul(psS[:NT, a, 0:4 * NT], ident16[:NT, :NT], bias[:, a, :],
                                             start=True, stop=False, skip_group_check=True)
                        for hh in range(4):
                            for a in range(2):
                                lo = 64 * a
                                mm = nc.tensor.matmul(psS[:NT, a, hh * NT:(hh + 1) * NT],
                                                      qkv[1 - u][lo:lo + 64, hh, s, :], qkv[1 - u][lo:lo + 64, QB + hh, s, :],
                                                      start=False, stop=True, skip_group_check=True)
                        mm.then_inc(s_mm, 1)
                    if f.proj:
                        proj(t, u, f, 3 * s + 1)
                    if f.tok:
                        tok_taps(t, s, 1, 2)
                    if f.attn and prev:
                        pe.wait_ge(v_evac, n + 1)
                    if f.scat and s == 0:
                        wait(pe, rw_done, t - 4)
                        wait(pe, a_evac, n - 1 if prev else B)
                        mm = nc.tensor.transpose(psRT, rw[:, :, :].rearrange("p b e -> p (b e)"),
                                                 ident[:NT, :NT])
                        if not prev:
                            mm.then_inc(rwT_tr, 1)
                    if prev:
                        pe.wait_ge(norm_done, n)
                        for j in range(QB):
                            mm = nc.tensor.transpose(psV[:, j * NT:(j + 1) * NT], attn[:, j * 128:(j + 1) * 128],
                                                     ident[:NT, :NT])
                        mm.then_inc(a_tr, 1)
                    if f.gate and s == 2:
                        wait(pe, hnT_evac, t - 3)
                        for b in range(GB):
                            mm = nc.tensor.matmul(psGate[:, b * E:(b + 1) * E], hnT[:, b * NT:(b + 1) * NT],
                                                  wgate[:, :], start=True, stop=True)
                        mm.then_inc(gate_mm, 1)
                    if f.gate and s == 3:
                        wait(pe, mask_done, t - 3)
                        nc.tensor.matmul(psRank[:, :], tri[:, :], mask[:, :], start=True, stop=False)
                        for b in range(GB - 1):
                            later = mask[:, b * E:(b + 1) * E].unsqueeze(1).broadcast_to([NT, GB - 1 - b, E])
                            nc.tensor.matmul(psRank[:, (b + 1) * E:].rearrange("p (b e) -> p b e", e=E), ones16[:, :NT], later,
                                             start=False, stop=(b == GB - 2))
                        for b in range(GB):
                            mm = nc.tensor.matmul(psTot, ones16[:, :], mask[:, b * E:(b + 1) * E],
                                                  start=(b == 0), stop=(b == GB - 1))
                        mm.then_inc(rank_mm, 1)
                    if f.tok:
                        tok_taps(t, s, 3, 1)
                    if f.proj:
                        proj(t, u, f, 3 * s + 2)
                    if prev:
                        pe.wait_ge(a_evac, n)
                        if f.gate and s == 3:
                            wait(pe, base_done, t - 3)
                        for j in range(QB):
                            mm = nc.tensor.matmul(psWout, attnT[:, j, :], wout[:, j, :],
                                                  start=(j == 0), stop=(j == QB - 1))
                        mm.then_inc(out_mm, 1)

            run(pe, step)

            pe.wait_ge(tcol_ready, 1)
            pe.wait_ge(rwT_evac, NG)
            for c in range(2):
                mm = nc.tensor.matmul(psTok[0:1, c * 128:(c + 1) * 128], tcol[:, c:c + 1], ident[:, :],
                                      start=True, stop=True)
            mm.then_inc(table_mm, 1)

            def turn(r, k):
                i = r * ROUND + k
                pe.wait_ge(xs_in[k % NR], r * (16 * ROUND // NR) + (16 * (k // NR) + 16))
                wait(pe, xs_evac, i - (NX - 1))
                nc.tensor.transpose(psX[k % NX][:, 0:128], xs[k % NR][:, :], ident[:, :]).then_inc(xs_tr, 1)

            def up(r, k):
                i = r * ROUND + k
                by_act = sum(copies(q) for q in range(k + 1))
                if copies(k):
                    pe.wait_ge(w_act_ready, r * len(BY_ACT) + by_act)
                else:
                    pe.wait_ge(w_dve_ready, r * (ROUND - len(BY_ACT)) + (k + 1 - by_act))
                pe.wait_ge(xs_evac, i + 1)
                wait(pe, silu_done, i - (NX - 1))
                for j in range(FB):
                    mm = nc.tensor.matmul(psUp[k % NX][:, j * 128:(j + 1) * 128], wtile[k % NX][:, j * 128:(j + 1) * 128],
                                          xsT[k % NX][:, :], start=True, stop=True)
                mm.then_inc(up_mm, 1)

            def tile(r, k):
                if exists(r * ROUND + (k + AHEAD)):
                    turn(r, k + AHEAD)
                up(r, k)

            for k in range(AHEAD):
                turn(0, k)
            run_tiles(pe, tile)

            pe.wait_ge(tile_sum, NTILE)
            pe.wait_ge(xs_evac, NTILE)
            for j in range(FB):
                mm = nc.tensor.transpose(psTok[:NTILE, j * 128:(j + 1) * 128], part[:, :, j], ident[:, :])
            mm.then_inc(part_tr, 1)
            pe.wait_ge(part_evac, 1)
            for j in range(FB):
                mm = nc.tensor.matmul(psV[:, j * E:(j + 1) * E], partT[:NTILE, j * 128:(j + 1) * 128],
                                      owner[:NTILE, :], start=True, stop=True)
            mm.then_inc(sum_mm, 1)
            pe.wait_ge(mean_ready, 1)
            pe.wait_ge(late_w_in, 16 * FB)
            for e in range(E - E_DVE):
                for j in range(FB):
                    nc.tensor.matmul(psTok[0:E, 0:D], mean[:, j, e * E:(e + 1) * E], w2s[j][:, e, :],
                                     start=(e == 0 and j == 0), stop=False)
            pe.wait_ge(unit_ready, 1)
            pe.wait_ge(acc_done, FB * E_DVE)
            for e in range(E - E_DVE, E):
                mm = nc.tensor.matmul(psTok[0:E, 0:D], unit[:, e * E:(e + 1) * E], acc[e - E][:, :],
                                      start=False, stop=(e == E - 1))
            mm.then_inc(down_mm, 1)
            pe.wait_ge(y_evac, 1)
            nc.tensor.matmul(psTok[:, 128:256], misc[0:E, C_REP:C_REP + 128], ysb[0:E, :], start=True,
                             stop=True).then_inc(y_rep, 1)
            pe.wait_ge(ymix_ready, 1)

            def mix(g, u):
                pe.wait_ge(rstage_done, g + 1)
                wait(pe, out_add, g - (NO - 1))
                nc.tensor.matmul(psOut[u], rstage[u][:, :], ymix[:, :, :].rearrange("p b d -> p (b d)"),
                                 start=True, stop=True).then_inc(mix_mm, 1)

            for g in range(NO):
                mix(g, g)
            with pe.Fori(1, NG // NO) as r:
                for u in range(NO):
                    mix(r * NO + u, u)

        @block.scalar
        def _(ac):
            for s in range(GB):
                ac.dma_start(wtok_raw[:, s, :, :], w_tok[:, s, :, :]).then_inc(tok_w_in[s], 16)

            def high(q, u):
                wait(ac, tap_mm, q - 1)
                nc.scalar.activation(x_hi[u][:, 0:PIECE], x_raw[u][:, :], ACT.Copy).then_inc(x_hi_done, 1)

            def tap2(t, u, k):
                wait(ac, proj_mm, (t - 2) * NBLK + (k + 1))
                if k == 0 and isinstance(t, int) and t == 2:
                    ac.wait_ge(taps_ready, 1)
                    ac.wait_ge(wqkv_lo_done, 1)
                nc.scalar.activation(qkv[u][:, k, :, :], psP[(k + 1) % 2][:, 0:GT].rearrange("p (b n) -> p b n", n=NT),
                                     ACT.Copy, scale=taps[:, k, 2:3]).then_inc(tap2_done, 1)

            ac.wait_ge(x_in[0], 16)
            high(0, 0)
            for s in range(GB):
                ac.wait_ge(tok_w_in[s], 16)
                nc.scalar.activation(wtok_hi[:, s, :, :], wtok_raw[:, s, :, :], ACT.Copy).then_inc(wtok_hi_done, 1)

            def normalise(g, rstd, shift, dst, s_shift, s_done):
                wait_apart(ac, s_shift, g + 1)
                for b in range(GB):
                    i = nc.scalar.activation(dst[:, b, :], resid[:, bass.ds(g * (GB * D) + b * D, D)], ACT.Identity,
                                             bias=shift[:, b:b + 1], scale=rstd[:, b:b + 1])
                i.then_inc(s_done, 1)

            def step(t, u, f):
                for s in range(GB):
                    n = (t - 3) * GB + s
                    prev = f.attn and s > 0 or f.last and s == 0
                    if prev:
                        wait(ac, pv_mm, n - 1)
                        for a in range(2):
                            ac.wait_ge(p_tr, n * 2 - 1 + a)
                            nc.scalar.activation(probT[:, a, :, :].rearrange("p h n -> p (h n)"),
                                                 psS[:NT, a, 0:4 * NT], ACT.Copy).then_inc(p_evac, 1)
                    if f.gate and s == 2:
                        wait(ac, hnT_tr, t - 3)
                        nc.scalar.activation(hnT[:, :], psHn, ACT.Copy).then_inc(hnT_evac, 1)
                    if f.attn:
                        ac.wait_ge(v_tr, n + 1)
                        wait(ac, pv_mm, n - 1)
                        if isinstance(t, int) and t == 3 and s == 0:
                            ac.wait_ge(vones_ready, 2)
                        nc.scalar.activation(vrow[s % 2][:, :, 0:DH],
                                             psV[:NT, :].rearrange("p (h d) -> p h d", d=DH), ACT.Copy)\
                            .then_inc(v_evac, 1)
                    if f.proj:
                        tap2(t, u, 3 * s)
                    if f.norm and s == 0:
                        wait(ac, tok_tr, t)
                        nc.scalar.activation(resid[:, bass.ds((t - 1) * (GB * D), GB * D)], psP[0][:NT, :],
                                             ACT.Copy).then_inc(res_evac, 1)
                    if f.norm and s == 3:
                        wait(ac, xnT_tr, t)
                        wait(ac, xnT_lo_done, t - 1)
                        nc.scalar.activation(xnT[:, :], psP[1][:, 0:GT], ACT.Identity, bias=bet[:, 0:1],
                                             scale=gam[:, 0:1]).then_inc(xnT_evac, 1)
                        wait(ac, xnT_evac, t)
                        nc.scalar.activation(xnT_hi[1 - u][:, :], xnT[:, :], ACT.Copy).then_inc(xnT_hi_done, 1)
                    if f.tok and f.more(t, s):
                        ac.wait_ge(x_in[(s + 1) % 2], t * (16 * GB // 2) + (16 * ((s + 1) // 2) + 16))
                        high(t * GB + (s + 1), (s + 1) % 2)
                    if f.norm and s == 2:
                        normalise(t - 1, rstd, shift, xn, ln_shift, xn_ready)
                    if f.gate and s == 1:
                        wait(ac, scattered[u], (t - u - 4) * (16 * GB))
                        normalise(t - 4, rstd2, shift2, hn[u], ln2_shift, hn_ready)
                    if f.proj:
                        tap2(t, u, 3 * s + 1)
                    if f.scat and s == 0:
                        if prev:
                            ac.wait_ge(a_tr, n)
                        else:
                            ac.wait_ge(rwT_tr, 1)
                        nc.scalar.activation(rwT[:, bass.ds((t - 5) * NT, NT)], psRT, ACT.Copy).then_inc(rwT_evac, 1)
                    if prev:
                        ac.wait_ge(a_tr, n)
                        wait(ac, out_mm, n - 1)
                        nc.scalar.activation(attnT[:, :, :].rearrange("p j n -> p (j n)"), psV[:, 0:GT],
                                             ACT.Copy).then_inc(a_evac, 1)
                    if f.attn:
                        ac.wait_ge(shift_done, n + 1)
                        shifted = prob[:, :, :, :].rearrange("p a h n -> p (a h n)")
                        nc.scalar.activation(shifted, shifted, ACT.Exp).then_inc(exp_done, 1)
                    if f.gate and s == 3:
                        wait(ac, gap_done, t - 3)
                        nc.scalar.activation(egap[:, :], gap[:, :], ACT.Exp).then_inc(egap_done, 1)
                    if f.proj:
                        tap2(t, u, 3 * s + 2)
                    if isinstance(t, int) and t == 0 and s == GB - 1:
                        ac.wait_ge(proj_w_in, 16 * 8)
                        nc.scalar.activation(wqkv_hi[:, :, :], wqkv_raw[:, :, :], ACT.Copy).then_inc(wqkv_hi_done, 1)
                        ac.wait_ge(small_in, 16 * 7)
                    if f.tok and s == GB - 1:
                        wait(ac, tap_mm, t * GB + GB)
                        wait(ac, tok_tr, t)
                        nc.scalar.activation(tokT[:, :].rearrange("p (b n) -> p b n", n=NT),
                                             psTok[:, 0:GM].rearrange("p (b n) -> p b n", n=MR)[:, :, 0:NT], ACT.Identity,
                                             bias=btok[:, 0:1]).then_inc(tok_evac, 1)

            run(ac, step)
            ac.wait_ge(tail_ready, 1)
            tails(ac, 1)

            def silu(i, k):
                ac.wait_ge(up_mm, i + 1)
                wait(ac, tile_sum, i - (NX - 1))
                nc.scalar.activation(act[k][:, :], psUp[k][:, :], ACT.Silu).then_inc(silu_done, 1)

            def xs_copy(i, k):
                ac.wait_ge(xs_tr, i + 1)
                wait(ac, up_mm, i - (NX - 1))
                nc.scalar.activation(xsT[k][:, :], psX[k][:, 0:128], ACT.Copy).then_inc(xs_evac, 1)

            def tile(r, k):
                i = r * ROUND + k
                if exists(i + AHEAD):
                    xs_copy(i + AHEAD, (k + AHEAD) % NX)
                silu(i, k % NX)
                if exists(i + NX) and copies(k + NX):
                    expert(ac, lambda d, w: nc.scalar.activation(d, w, ACT.Copy), i + NX, k + NX, w_act_ready)

            ac.wait_ge(table_ready, 1)
            ac.wait_ge(expert_w_in, 16 * 2 * GB)
            for k in range(NX):
                if copies(k):
                    expert(ac, lambda d, w: nc.scalar.activation(d, w, ACT.Copy), k, k, w_act_ready)
            for k in range(AHEAD):
                xs_copy(k, k)
            run_tiles(ac, tile)

            def stage(g, u):
                wait(ac, mix_mm, g - (NO - 1))
                nc.scalar.activation(rstage[u][:, :], rwT[:, bass.ds(g * NT, NT)], ACT.Copy).then_inc(rstage_done, 1)

            ac.wait_ge(rwT_evac, NG)
            for g in range(NO):
                stage(g, g)
            with ac.Fori(1, NG // NO) as r:
                for u in range(NO):
                    stage(r * NO + u, u)

        @block.vector
        def _(dve):
            for u in range(2):
                nc.vector.memset(vrow[u][:, :, DH:DH + 1], 1.0).then_inc(vones_ready, 1)
            nc.vector.memset(zeros[:, :], 0.0).then_inc(zeros_ready, 1)
            nc.vector.memset(rw[:, :, :], 0.0).then_inc(rwzero_ready, 1)
            dve.wait_ge(zeros_ready, 1)
            for buf in x_hi + x_lo:
                nc.vector.tensor_copy(buf[:, PIECE:PIECE + 2], zeros[:, 0:2]).then_inc(pads_ready, 1)
            for s in range(GB):
                dve.wait_ge(wtok_hi_done, s + 1)
                nc.vector.tensor_tensor(wtok_lo[:, s, :, :], wtok_raw[:, s, :, :], wtok_hi[:, s, :, :].bitcast(F32),
                                        ALU.subtract).then_inc(wtok_lo_done, 1)
            dve.wait_ge(small_in, 16 * 7)
            nc.vector.tensor_copy(base[0][:, :], misc[:, C_BASE:C_BASE + E]).then_inc(consts_ready, 1)
            dve.wait_ge(proj_w_in, 16 * 8)
            nc.vector.tensor_scalar(taps[:, 0:QB, :], taps[:, 0:QB, :], float(DH) ** -0.5, None,
                                    ALU.mult).then_inc(taps_ready, 1)
            dve.wait_ge(wqkv_hi_done, 1)
            nc.vector.tensor_tensor(wqkv_lo[:, :, :], wqkv_raw[:, :, :], wqkv_hi[:, :, :].bitcast(F32), ALU.subtract)\
                .then_inc(wqkv_lo_done, 1)
            dve.wait_ge(taps_ready, 1)
            dve.wait_ge(rwzero_ready, 1)
            dve.wait_ge(consts_ready, 1)

            def conv(t, u, k):
                src = psP[(k + 1) % 2][:, 0:GT].rearrange("p (b n) -> p b n", n=NT)
                dst = qkv[u][:, k, :, :]
                wait(dve, tap2_done, (t - 2) * NBLK + (k + 1))
                nc.vector.scalar_tensor_tensor(dst[:, :, 1:NT], src[:, :, 0:NT - 1], taps[:, k, 1:2], dst[:, :, 1:NT],
                                               ALU.mult, ALU.add).then_inc(tap1_done, 1)
                wait(dve, tap1_done, (t - 2) * NBLK + (k + 1))
                nc.vector.scalar_tensor_tensor(dst[:, :, 2:NT], src[:, :, 0:NT - 2], taps[:, k, 0:1], dst[:, :, 2:NT],
                                               ALU.mult, ALU.add).then_inc(conv_done, 1)

            def stats(g, stat, mv, s_stat, s_mv):
                for b in range(GB):
                    i = nc.vector.bn_stats(stat[:, b, :], resid[:, bass.ds(g * (GB * D) + b * D, D)])
                i.then_inc(s_stat, 1)
                wait_apart(dve, s_stat, g + 1)
                for b in range(GB):
                    i = nc.vector.bn_aggr(mv[:, b, :], stat[:, b, :])
                i.then_inc(s_mv, 1)

            def step(t, u, f):
                for s in range(GB):
                    n = (t - 3) * GB + s
                    prev = f.attn and s > 0 or f.last and s == 0
                    if f.scat and s == 0:
                        place(t - 5, 1 - u)
                    if f.gate and s == 1:
                        wait(dve, res_add, (t - 3) * GB)
                        stats(t - 4, stat2, mv2, ln2_stat, ln2_mv)
                    if f.gate and s == 3:
                        choose(t - 4)
                    if f.norm and s == 2:
                        wait(dve, res_evac, t)
                        stats(t - 1, stat, mv, ln_stat, ln_mv)
                    if f.proj:
                        conv(t, u, 3 * s)
                    if prev:
                        o = heads(psO, DH + 1)
                        dve.wait_ge(pv_mm, n)
                        nc.vector.reciprocal(rden[:, :, :], o[:, :, :, DH]).then_inc(den_done, 1)
                        dve.wait_ge(den_done, n)
                        wait(dve, a_tr, n - 1)
                        nc.vector.tensor_tensor(attn[:, :].rearrange("p (a h d) -> p a h d", a=2, d=DH),
                                                o[:, :, :, 0:DH],
                                                rden[:, :, :].unsqueeze(3).broadcast_to([NT, 2, 4, DH]),
                                                ALU.mult).then_inc(norm_done, 1)
                    if f.attn:
                        dve.wait_ge(s_mm, n + 1)
                        nc.vector.tensor_reduce(rmax[:, :, :], heads(psS, NT), AXX, ALU.max).then_inc(max_done, 1)
                        dve.wait_ge(max_done, n + 1)
                        wait(dve, p_tr, n * 2)
                        nc.vector.tensor_tensor(prob[:, :, :, :], heads(psS, NT),
                                                rmax[:, :, :].unsqueeze(3).broadcast_to([NT, 2, 4, NT]),
                                                ALU.subtract).then_inc(shift_done, 1)
                    if f.gate and s == 3:
                        rank(t - 4, u)
                    if f.proj:
                        conv(t, u, 3 * s + 1)
                    if f.proj:
                        conv(t, u, 3 * s + 2)
                    if prev:
                        dve.wait_ge(out_mm, n)
                        res = resid[:, bass.ds((n - 1) * D, D)]
                        nc.vector.tensor_tensor(res, psWout, res, ALU.add).then_inc(res_add, 1)
                    if f.gate and s == 2:
                        route(t - 4)

            def route(g):
                wait(dve, gate_mm, g + 1)
                nc.vector.tensor_copy(logit[:, :, :].rearrange("p b e -> p (b e)"), psGate).then_inc(logit_copy, 1)
                wait_apart(dve, logit_copy, g + 1)
                for b in range(GB):
                    i = nc.vector.max(top[:, b, :], logit[:, b, :])
                i.then_inc(top_done, 1)
                wait_apart(dve, top_done, g + 1)
                for b in range(GB):
                    i = nc.vector.max_index(topi[:, b, :], top[:, b, :], logit[:, b, :])
                i.then_inc(topi_done, 1)
                nc.vector.tensor_tensor(gap[:, :], top[:, :, 1], top[:, :, 0], ALU.subtract).then_inc(gap_done, 1)

            def choose(g):
                wait(dve, topi_done, g + 1)
                nc.vector.tensor_copy(idxf[:, :, :], topi[:, :, 0:2].rearrange("p b k -> p k b")).then_inc(idxf_done, 1)
                wait(dve, idxf_done, g + 1)
                nc.vector.tensor_tensor(hot[:, :, :], iota.unsqueeze(1).broadcast_to([NT, 2 * GB, E]),
                                        idxf[:, :, :].rearrange("p k b -> p (k b)").unsqueeze(2)
                                        .broadcast_to([NT, 2 * GB, E]), ALU.is_equal).then_inc(hot_done, 1)
                wait(dve, hot_done, g + 1)
                nc.vector.tensor_tensor(mask[:, :].rearrange("p (b e) -> p b e", e=E), hot[:, 0:GB, :],
                                        hot[:, GB:, :], ALU.add).then_inc(mask_done, 1)

            def rank(g, u):
                wait(dve, rank_mm, g + 1)
                was = base[u]
                nc.vector.tensor_tensor(pos[:, :].rearrange("p (b e) -> p b e", e=E),
                                        psRank.rearrange("p (b e) -> p b e", e=E),
                                        was[:NT, :].unsqueeze(1).broadcast_to([NT, GB, E]), ALU.add)\
                    .then_inc(pos_done, 1)
                nc.vector.tensor_tensor(base[1 - u][:, :], was[:, :], psTot, ALU.add).then_inc(base_done, 1)

            def place(g, u):
                wait(dve, egap_done, g + 1)
                nc.vector.tensor_scalar(wden[:, :], egap[:, :], 1.0, None, ALU.add).then_inc(wden_done, 1)
                wait(dve, wden_done, g + 1)
                nc.vector.reciprocal(wts[:, 0, :], wden[:, :]).then_inc(w0_done, 1)
                wait(dve, pos_done, g + 1)
                nc.vector.tensor_tensor(sel[:, :, :].rearrange("p (k b) e -> p k (b e)", k=2),
                                        hot[:, :, :].rearrange("p (k b) e -> p k (b e)", k=2),
                                        pos[:, :].unsqueeze(1).broadcast_to([NT, 2, GB * E]), ALU.mult)\
                    .then_inc(sel_done, 1)
                wait(dve, w0_done, g + 1)
                nc.vector.tensor_tensor(wts[:, 1, :], egap[:, :], wts[:, 0, :], ALU.mult).then_inc(w1_done, 1)
                wait(dve, sel_done, g + 1)
                nc.vector.tensor_reduce(slotf[:, :], sel[:, :, :], AXX, ALU.add).then_inc(slotf_done, 1)
                wait(dve, w1_done, g + 1)
                nc.vector.tensor_tensor(wsel[:, :, :], hot[:, :, :],
                                        wts[:, :, :].rearrange("p k b -> p (k b)").unsqueeze(2)
                                        .broadcast_to([NT, 2 * GB, E]), ALU.mult).then_inc(wsel_done, 1)
                wait(dve, slotf_done, g + 1)
                nc.vector.tensor_copy(slot[u][:, :], slotf[:, :]).then_inc(slot_done, 1)
                wait(dve, wsel_done, g + 1)
                wait(dve, rwT_evac, g)
                nc.vector.tensor_tensor(rw[:, :, 0:E], wsel[:, 0:GB, :], wsel[:, GB:, :], ALU.add).then_inc(rw_done, 1)
                wait(dve, base_done, g + 1)

            run(dve, step)

            steps = [0]

            def link(ins):
                steps[0] += 1
                ins.then_inc(dve_step, 1)
                dve.wait_ge(dve_step, steps[0])

            last = base[NG % 2]
            nc.vector.tensor_copy(taili[:, :], last[0:1, :]).then_inc(tail_ready, 1)
            link(nc.vector.tensor_tensor(cnt[:, :], last[:, :], misc[:, C_BASE:C_BASE + E], ALU.subtract))
            link(nc.vector.tensor_scalar(cnti[:, :], cnt[:, :], 127.0, None, ALU.add))
            link(nc.vector.tensor_scalar(cntt[:, :], cnti[:, :], 7, None, ALU.arith_shift_right))
            link(nc.vector.tensor_copy(ntl[:, :], cntt[:, :]))
            link(nc.vector.memset(ones[:, :], 1.0))
            link(nc.vector.tensor_tensor_scan(tend[:, :], ones[:, :], ntl[:, :], 0.0, ALU.mult, ALU.add))
            link(nc.vector.tensor_scalar(past[:, :], tend[:, :], misc[:, C_TILE:C_TILE + 1], None, ALU.is_le))
            link(nc.vector.tensor_reduce(tcol[:, 3:4], past[:, :], AXX, ALU.add))
            link(nc.vector.tensor_tensor(pastt[:, :], past[:, :], tend[:, :], ALU.mult))
            link(nc.vector.tensor_reduce(tcol[:, 4:5], pastt[:, :], AXX, ALU.max))
            link(nc.vector.tensor_scalar(tcol[:, 5:6], tcol[:, 3:4], float(E), 128.0, ALU.is_lt, ALU.mult))
            link(nc.vector.tensor_tensor(tcol[:, 6:7], misc[:, C_TILE:C_TILE + 1], tcol[:, 4:5], ALU.subtract))
            link(nc.vector.tensor_tensor(tcol[:, 6:7], tcol[:, 6:7], tcol[:, 5:6], ALU.mult))
            link(nc.vector.tensor_scalar(tcol[:, 0:1], tcol[:, 3:4], float(CAP), tcol[:, 6:7], ALU.mult, ALU.add))
            link(nc.vector.tensor_scalar(tcol[:, 2:3], tcol[:, 3:4], float(E - 1), None, ALU.min))
            link(nc.vector.tensor_scalar(tcol[:, 1:2], tcol[:, 2:3], float(F), None, ALU.mult))
            link(nc.vector.tensor_scalar(owner[:, :], misc[:, C_IOTA:C_IOTA + E], tcol[:, 2:3], None, ALU.is_equal))
            nc.vector.tensor_scalar(invc[:, :], cnt[:, :], 1.0, None, ALU.max).then_inc(tcol_ready, 1)
            dve.wait_ge(tcol_ready, 1)
            dve.wait_ge(table_mm, 1)
            link(nc.vector.reciprocal(invc[:, :], invc[:, :]))
            nc.vector.tensor_copy(tab[:, :], psTok[0:1, 0:2 * 128]).then_inc(table_ready, 1)

            def tile_total(i, k):
                wait_apart(dve, silu_done, i + 1)
                nc.vector.tensor_reduce(part[:, bass.ds(i, 1), :].rearrange("p i j -> p (i j)"),
                                        act[k][:, :].rearrange("p (j n) -> p j n", n=128), AXX, ALU.add)\
                    .then_inc(tile_sum, 1)

            nc.vector.memset(unit[:, :], 0.0).then_inc(unit_zero, 1)
            dve.wait_ge(unit_zero, 1)
            nc.vector.memset(unit[:, 0:E * E:E + 1], 1.0).then_inc(unit_ready, 1)
            link(nc.vector.memset(mean[:, :, :], 0.0))
            dve.wait_ge(table_ready, 1)
            dve.wait_ge(expert_w_in, 16 * 2 * GB)
            for k in range(NX):
                if not copies(k):
                    expert(dve, nc.vector.tensor_copy, k, k, w_dve_ready)

            def tile(r, k):
                i = r * ROUND + k
                tile_total(i, k % NX)
                if exists(i + NX) and not copies(k + NX):
                    expert(dve, nc.vector.tensor_copy, i + NX, k + NX, w_dve_ready)

            run_tiles(dve, tile)
            dve.wait_ge(part_tr, 1)
            nc.vector.tensor_copy(partT[:NTILE, :], psTok[:NTILE, :]).then_inc(part_evac, 1)
            dve.wait_ge(sum_mm, 1)
            nc.vector.tensor_tensor(mean[:, :, 0:E * E:E + 1], psV[:, 0:FB * E].rearrange("p (j e) -> p j e", e=E),
                                    invc[:, :].unsqueeze(1).broadcast_to([128, FB, E]), ALU.mult)\
                .then_inc(mean_ready, 1)
            dve.wait_ge(mean_ready, 1)
            dve.wait_ge(late_w_in, 16 * FB)
            for j in range(FB):
                if j:
                    dve.wait_ge(acc_done, j * E_DVE)
                for e in range(E - E_DVE, E):
                    part_mean = mean[:, j, e * E + e:e * E + e + 1]
                    if j == 0:
                        i = nc.vector.tensor_scalar(acc[e - E][:, :], w2s[j][:, e, :], part_mean, None, ALU.mult)
                    else:
                        i = nc.vector.scalar_tensor_tensor(acc[e - E][:, :], w2s[j][:, e, :], part_mean,
                                                           acc[e - E][:, :], ALU.mult, ALU.add)
                    i.then_inc(acc_done, 1)
            dve.wait_ge(down_mm, 1)
            nc.vector.tensor_copy(ysb[0:E, :], psTok[0:E, 0:D]).then_inc(y_evac, 1)
            dve.wait_ge(y_rep, 1)
            nc.vector.tensor_tensor(ymix[:, :, :], psTok[:, 128:256].unsqueeze(1).broadcast_to([128, GB, D]),
                                    misc[:, C_BLK:C_BLK + GB].unsqueeze(2).broadcast_to([128, GB, D]), ALU.mult)\
                .then_inc(ymix_ready, 1)

            def finish(g, u, first=False):
                dve.wait_ge(mix_mm, g + 1)
                if not first:
                    dve.wait_ge(out_done[u], (g - u) * (16 // NO))
                nc.vector.tensor_tensor(osb[u][:, :], psOut[u], resid[:, bass.ds(g * (GB * D), GB * D)],
                                        ALU.add).then_inc(out_add, 1)

            for g in range(NO):
                finish(g, g, True)
            with dve.Fori(1, NG // NO) as r:
                for u in range(NO):
                    finish(r * NO + u, u)

        @block.gpsimd
        def _(pool):
            def low(q, u):
                pool.wait_ge(x_hi_done, q + 1)
                nc.gpsimd.tensor_tensor(x_lo[u][:, 0:PIECE], x_raw[u][:, :], x_hi[u][:, 0:PIECE].bitcast(F32), ALU.subtract)\
                    .then_inc(x_lo_done, 1)

            def constants():
                pool.wait_ge(small_in, 16 * 7)
                nc.gpsimd.tensor_copy(bias[:, :, :].rearrange("p a n -> p (a n)"), bias32[:, :]).then_inc(bias_cast, 1)
                nc.gpsimd.tensor_copy(ident16[:, :], ident[:, :]).then_inc(bias_cast, 1)
                nc.gpsimd.tensor_copy(tri[:, :], tri32[:, :]).then_inc(bias_cast, 1)
                nc.gpsimd.memset(ones16[:, :], 1.0).then_inc(bias_cast, 1)

            nc.gpsimd.memset(half[:, :], -0.5).then_inc(half_ready, 1)
            pool.wait_ge(half_ready, 1)
            low(0, 0)

            def step(t, u, f):
                for s in range(GB):
                    if f.norm and s == 2:
                        wait_apart(pool, ln_mv, t)
                        nc.gpsimd.tensor_scalar(veps[:, :], mv[:, :, 1], 1.0 + EPS, EPS * EPS, ALU.mult, ALU.add)\
                            .then_inc(ln_veps, 1)
                        nc.gpsimd.tensor_scalar(nmean[:, :], mv[:, :, 0], -1.0, 0.0, ALU.mult, ALU.add)\
                            .then_inc(ln_nmean, 1)
                        wait(pool, ln_veps, t)
                        nc.gpsimd.tensor_tensor(rstd[:, :], veps[:, :], half[:, :], ALU.pow).then_inc(ln_rstd, 1)
                        wait(pool, ln_rstd, t)
                        wait(pool, ln_nmean, t)
                        nc.gpsimd.tensor_tensor(shift[:, :], nmean[:, :], rstd[:, :], ALU.mult).then_inc(ln_shift, 1)
                    if f.gate and s == 1:
                        wait_apart(pool, ln2_mv, t - 3)
                        nc.gpsimd.tensor_scalar(veps2[:, :], mv2[:, :, 1], 1.0, EPS, ALU.mult, ALU.add)\
                            .then_inc(ln2_veps, 1)
                        nc.gpsimd.tensor_scalar(nmean2[:, :], mv2[:, :, 0], -1.0, 0.0, ALU.mult, ALU.add)\
                            .then_inc(ln2_nmean, 1)
                        wait(pool, ln2_veps, t - 3)
                        nc.gpsimd.tensor_tensor(rstd2[:, :], veps2[:, :], half[:, :], ALU.pow).then_inc(ln2_rstd, 1)
                        wait(pool, ln2_rstd, t - 3)
                        wait(pool, ln2_nmean, t - 3)
                        nc.gpsimd.tensor_tensor(shift2[:, :], nmean2[:, :], rstd2[:, :], ALU.mult).then_inc(ln2_shift, 1)
                    if f.tok and f.more(t, s):
                        low(t * GB + (s + 1), (s + 1) % 2)
                    if isinstance(t, int) and t == 2 and s == 0:
                        constants()
                    if isinstance(t, int) and 1 <= t <= 2:
                        c = (t - 1) * GB + s
                        nc.gpsimd.dma_start(w1s[:, c * W1P:(c + 1) * W1P], w1[:, c * W1P:(c + 1) * W1P])\
                            .then_inc(expert_w_in, 16)
                    if f.norm and s == 3:
                        wait(pool, xnT_hi_done, t)
                        nc.gpsimd.tensor_tensor(xnT_lo[1 - u][:, :], xnT[:, :], xnT_hi[1 - u][:, :].bitcast(F32), ALU.subtract)\
                            .then_inc(xnT_lo_done, 1)
                    if f.scat and s == 2:
                        scatter(t - 5, u)

            def scatter(g, u):
                wait_apart(pool, slot_done, g + 1)
                for k in range(2):
                    for b in range(GB):
                        c = k * GB + b
                        nc.gpsimd.indirect_dma_start(
                            rows, bass.IndirectOffsetOnAxis(slot[1 - u][:, c:c + 1], 0), hn[1 - u][:, b, :], None)\
                            .then_inc(scattered[1 - u], 16)

            run(pool, step)
            fetch_tiles(pool, 1)

    return nc


def kernel(**inputs):
    import numpy as np
    import concourse.bacc as bacc
    from concourse.bass_utils import run_bass_kernel_spmd

    x = np.asarray(inputs["x"])
    padded = np.zeros((B, MR * S, D), x.dtype)
    padded[:, :T] = x

    def w(name):
        return np.asarray(inputs[name])

    def blocks(a):
        return a.T.reshape(D, QB, 128)

    def tapcols(a):
        return a.reshape(QB, 128, 3).transpose(1, 0, 2)

    i, j = np.arange(NT)[:, None], np.arange(NT)[None, :]
    alibi = np.stack([np.where(j <= i, (j - i) * 0.5 ** (h + 1), -1e30) for a in range(2) for h in range(a, H, 2)], 1)
    misc = np.zeros((128, C_END), np.float32)
    misc[:, C_IOTA:C_IOTA + E] = np.arange(E)
    misc[:, C_BASE:C_BASE + E] = np.arange(E) * CAP
    misc[:, C_TILE] = np.arange(128)
    misc[:, C_BLK:C_BLK + GB] = np.arange(128)[:, None] // ESTRIDE == np.arange(GB)
    misc[:E, C_REP:C_REP + 128] = np.arange(128)[None, :] % ESTRIDE == np.arange(E)[:, None]

    data = {
        "x": padded.reshape(NG, GB, MR, S, D).transpose(4, 0, 3, 1, 2).reshape(D, B * S * MR),
        "w_tok": w("L0_tok_W").reshape(D, D, 2, GB, 2).transpose(1, 3, 4, 2, 0).reshape(D, GB, 4, D),
        "b_tok": w("L0_tok_b").reshape(D, 1),
        "gamma": w("L0_attn_gamma").reshape(D, 1),
        "beta": w("L0_attn_beta").reshape(D, 1),
        "wq": blocks(w("L0_attn_wq1")), "wk": blocks(w("L0_attn_wk1")), "wv": blocks(w("L0_attn_wv1")),
        "cq": tapcols(w("L0_attn_wqd")), "ck": tapcols(w("L0_attn_wkd")), "cv": tapcols(w("L0_attn_wvd")),
        "w_out": w("L0_attn_wout").T.reshape(QB, 128, D).transpose(1, 0, 2),
        "w_gate": w("L0_ffn_gate_weight").T,
        "w1": w("L0_ffn_w1").transpose(2, 0, 1).reshape(D, E * F),
        "w2": w("L0_ffn_w2").reshape(E, D, FB, 128).transpose(3, 2, 0, 1),
        "c_ident": np.eye(128, dtype=np.float32),
        "c_bias": alibi.reshape(NT, 2 * GT).astype(np.float32),
        "c_tri": (i < j).astype(np.float32),
        "c_misc": misc,
    }
    nc = bacc.Bacc("TRN2", target_bir_lowering=False, num_devices=1)
    arrays, args = {}, []
    for name, a in data.items():
        a = np.ascontiguousarray(a)
        arrays[f"in_{name}"] = a
        args.append(nc.dram_tensor(f"in_{name}", a.shape, mybir.dt.from_np(a.dtype), kind="ExternalInput").ap())
    args.append(nc.dram_tensor("out_0", (B, NT, D), F32, kind="ExternalOutput").ap())
    build(nc, *args)
    r = run_bass_kernel_spmd(nc, [arrays], core_ids=[0])
    return r.results[0]["out_0"]
```
